# Optimizing a Trainium2 kernel written in Bass

```python
import numpy as np
import jax
import jax.numpy as jnp

def _softmax(x, axis=-1):
    return jax.nn.softmax(x, axis=axis)

def _gelu(x):
    return jax.nn.gelu(x, approximate=True)

def _silu(x):
    return jax.nn.silu(x)

def _sigmoid(x):
    return jax.nn.sigmoid(x)

def _layernorm(x, axis=-1, eps=1e-05):
    m = jnp.mean(x, axis=axis, keepdims=True)
    v = jnp.var(x, axis=axis, keepdims=True)
    return (x - m) / jnp.sqrt(v + eps)

def _scatter_add(tgt, idx, src, axis=0):
    return tgt.at[idx].add(src)

def _segment_sum(src, seg, n):
    return jax.ops.segment_sum(src, seg, n)
kernel_name = 'mk_dlrm_tower_d1_rec_r8_49ab0d'

def setup_inputs(seed: int=0):
    np.random.seed(seed)
    _w = jnp.asarray

    def _rec_inputs():
        import jax
        import jax.numpy as jnp
        _tk = jax.random.key(seed)
        ids = jnp.stack([jax.random.randint(jax.random.fold_in(_tk, 200 + f), (2048,), 0, v, jnp.int32) for f, v in enumerate([12500, 12500, 1250, 1250, 1250, 12500, 1000, 12500, 1250, 1000, 1250, 1250, 12500, 125000, 1000, 1000, 12500, 1000, 1000, 1000, 12500, 1000, 1250, 1000, 12500, 1250])], axis=1)
        tbl_0 = 0.05 * jax.random.normal(jax.random.fold_in(_tk, 500 + 0), (12500, 128), jnp.float32)
        tbl_1 = 0.05 * jax.random.normal(jax.random.fold_in(_tk, 500 + 1), (12500, 128), jnp.float32)
        tbl_2 = 0.05 * jax.random.normal(jax.random.fold_in(_tk, 500 + 2), (1250, 128), jnp.float32)
        tbl_3 = 0.05 * jax.random.normal(jax.random.fold_in(_tk, 500 + 3), (1250, 128), jnp.float32)
        tbl_4 = 0.05 * jax.random.normal(jax.random.fold_in(_tk, 500 + 4), (1250, 128), jnp.float32)
        tbl_5 = 0.05 * jax.random.normal(jax.random.fold_in(_tk, 500 + 5), (12500, 128), jnp.float32)
        tbl_6 = 0.05 * jax.random.normal(jax.random.fold_in(_tk, 500 + 6), (1000, 128), jnp.float32)
        tbl_7 = 0.05 * jax.random.normal(jax.random.fold_in(_tk, 500 + 7), (12500, 128), jnp.float32)
        tbl_8 = 0.05 * jax.random.normal(jax.random.fold_in(_tk, 500 + 8), (1250, 128), jnp.float32)
        tbl_9 = 0.05 * jax.random.normal(jax.random.fold_in(_tk, 500 + 9), (1000, 128), jnp.float32)
        tbl_10 = 0.05 * jax.random.normal(jax.random.fold_in(_tk, 500 + 10), (1250, 128), jnp.float32)
        tbl_11 = 0.05 * jax.random.normal(jax.random.fold_in(_tk, 500 + 11), (1250, 128), jnp.float32)
        tbl_12 = 0.05 * jax.random.normal(jax.random.fold_in(_tk, 500 + 12), (12500, 128), jnp.float32)
        tbl_13 = 0.05 * jax.random.normal(jax.random.fold_in(_tk, 500 + 13), (125000, 128), jnp.float32)
        tbl_14 = 0.05 * jax.random.normal(jax.random.fold_in(_tk, 500 + 14), (1000, 128), jnp.float32)
        tbl_15 = 0.05 * jax.random.normal(jax.random.fold_in(_tk, 500 + 15), (1000, 128), jnp.float32)
        tbl_16 = 0.05 * jax.random.normal(jax.random.fold_in(_tk, 500 + 16), (12500, 128), jnp.float32)
        tbl_17 = 0.05 * jax.random.normal(jax.random.fold_in(_tk, 500 + 17), (1000, 128), jnp.float32)
        tbl_18 = 0.05 * jax.random.normal(jax.random.fold_in(_tk, 500 + 18), (1000, 128), jnp.float32)
        tbl_19 = 0.05 * jax.random.normal(jax.random.fold_in(_tk, 500 + 19), (1000, 128), jnp.float32)
        tbl_20 = 0.05 * jax.random.normal(jax.random.fold_in(_tk, 500 + 20), (12500, 128), jnp.float32)
        tbl_21 = 0.05 * jax.random.normal(jax.random.fold_in(_tk, 500 + 21), (1000, 128), jnp.float32)
        tbl_22 = 0.05 * jax.random.normal(jax.random.fold_in(_tk, 500 + 22), (1250, 128), jnp.float32)
        tbl_23 = 0.05 * jax.random.normal(jax.random.fold_in(_tk, 500 + 23), (1000, 128), jnp.float32)
        tbl_24 = 0.05 * jax.random.normal(jax.random.fold_in(_tk, 500 + 24), (12500, 128), jnp.float32)
        tbl_25 = 0.05 * jax.random.normal(jax.random.fold_in(_tk, 500 + 25), (1250, 128), jnp.float32)
        _rk = jax.random.fold_in(_tk, 7)
        r_dense_features = -0.000520686 + 1.00062 * jax.random.normal(jax.random.fold_in(_rk, 101), (2048, 128), jnp.float32)
        W_top1 = 0.0405887 * jax.random.normal(jax.random.fold_in(_tk, 801), (607, 512), jnp.float32)
        W_top2 = 0.0441942 * jax.random.normal(jax.random.fold_in(_tk, 802), (512, 256), jnp.float32)
        W_top3 = 0.0625 * jax.random.normal(jax.random.fold_in(_tk, 803), (256, 1), jnp.float32)
        b_top1 = jnp.zeros((512,), jnp.float32)
        b_top2 = jnp.zeros((256,), jnp.float32)
        return (r_dense_features, ids, tbl_0, tbl_1, tbl_2, tbl_3, tbl_4, tbl_5, tbl_6, tbl_7, tbl_8, tbl_9, tbl_10, tbl_11, tbl_12, tbl_13, tbl_14, tbl_15, tbl_16, tbl_17, tbl_18, tbl_19, tbl_20, tbl_21, tbl_22, tbl_23, tbl_24, tbl_25, W_top1, b_top1, W_top2, b_top2, W_top3)
    r_dense_features, ids, tbl_0, tbl_1, tbl_2, tbl_3, tbl_4, tbl_5, tbl_6, tbl_7, tbl_8, tbl_9, tbl_10, tbl_11, tbl_12, tbl_13, tbl_14, tbl_15, tbl_16, tbl_17, tbl_18, tbl_19, tbl_20, tbl_21, tbl_22, tbl_23, tbl_24, tbl_25, W_top1, b_top1, W_top2, b_top2, W_top3 = _rec_inputs()

    def _L0_rec_setup():
        import jax, jax.numpy as jnp
        import numpy as np
        NUM_SPARSE = 26
        EMBED_DIM = 128
        BATCH = 2048
        key = jax.random.key(seed)
        k1, k2 = jax.random.split(key)
        dense_features = jax.random.normal(k1, (BATCH, EMBED_DIM), dtype=jnp.float32)
        sparse_features = jax.random.normal(k2, (BATCH, NUM_SPARSE, EMBED_DIM), dtype=jnp.float32)
        return {'dense_features': dense_features, 'sparse_features': sparse_features}
    _L0_rec_all = _L0_rec_setup()
    _L0_rec_in = {k: v for k, v in _L0_rec_all.items() if k in ()}
    del _L0_rec_all
    return {'r_dense_features': r_dense_features, 'ids': ids, 'tbl_0': tbl_0, 'tbl_1': tbl_1, 'tbl_2': tbl_2, 'tbl_3': tbl_3, 'tbl_4': tbl_4, 'tbl_5': tbl_5, 'tbl_6': tbl_6, 'tbl_7': tbl_7, 'tbl_8': tbl_8, 'tbl_9': tbl_9, 'tbl_10': tbl_10, 'tbl_11': tbl_11, 'tbl_12': tbl_12, 'tbl_13': tbl_13, 'tbl_14': tbl_14, 'tbl_15': tbl_15, 'tbl_16': tbl_16, 'tbl_17': tbl_17, 'tbl_18': tbl_18, 'tbl_19': tbl_19, 'tbl_20': tbl_20, 'tbl_21': tbl_21, 'tbl_22': tbl_22, 'tbl_23': tbl_23, 'tbl_24': tbl_24, 'tbl_25': tbl_25, 'W_top1': W_top1, 'b_top1': b_top1, 'W_top2': W_top2, 'b_top2': b_top2, 'W_top3': W_top3}

def reference(r_dense_features, ids, tbl_0, tbl_1, tbl_2, tbl_3, tbl_4, tbl_5, tbl_6, tbl_7, tbl_8, tbl_9, tbl_10, tbl_11, tbl_12, tbl_13, tbl_14, tbl_15, tbl_16, tbl_17, tbl_18, tbl_19, tbl_20, tbl_21, tbl_22, tbl_23, tbl_24, tbl_25, W_top1, b_top1, W_top2, b_top2, W_top3):
    import jax
    import jax.numpy as jnp

    def _L0_rec_ref(dense_features, sparse_features):
        import jax, jax.numpy as jnp
        import numpy as np
        NUM_SPARSE = 26
        EMBED_DIM = 128
        BATCH = 2048
        F = NUM_SPARSE + 1
        combined = jnp.concatenate([dense_features[:, None, :], sparse_features], axis=1)
        interactions = jnp.einsum('bfd,bgd->bfg', combined, combined)
        iu, ju = jnp.triu_indices(F, k=1)
        interactions_flat = interactions[:, iu, ju]
        return jnp.concatenate([dense_features, interactions_flat], axis=1)
    e = jnp.stack([tbl_0[ids[:, 0]], tbl_1[ids[:, 1]], tbl_2[ids[:, 2]], tbl_3[ids[:, 3]], tbl_4[ids[:, 4]], tbl_5[ids[:, 5]], tbl_6[ids[:, 6]], tbl_7[ids[:, 7]], tbl_8[ids[:, 8]], tbl_9[ids[:, 9]], tbl_10[ids[:, 10]], tbl_11[ids[:, 11]], tbl_12[ids[:, 12]], tbl_13[ids[:, 13]], tbl_14[ids[:, 14]], tbl_15[ids[:, 15]], tbl_16[ids[:, 16]], tbl_17[ids[:, 17]], tbl_18[ids[:, 18]], tbl_19[ids[:, 19]], tbl_20[ids[:, 20]], tbl_21[ids[:, 21]], tbl_22[ids[:, 22]], tbl_23[ids[:, 23]], tbl_24[ids[:, 24]], tbl_25[ids[:, 25]]], axis=1)
    z = _L0_rec_ref(r_dense_features, e)
    z = z.reshape(z.shape[0], -1)
    h = jnp.concatenate([z, r_dense_features], axis=1)
    h = jnp.maximum(h @ W_top1 + b_top1, 0.0)
    h = jnp.maximum(h @ W_top2 + b_top2, 0.0)
    y = h @ W_top3
    return y

_drawn_inputs = setup_inputs


def setup_inputs(seed=0):
    import zlib

    import numpy as np

    out = dict(_drawn_inputs(seed))
    spreads = {'b_top1': (0.0, 0.1), 'b_top2': (0.0, 0.1)}
    factors = {}
    for name, (base, spread) in spreads.items():
        noise = np.random.default_rng([zlib.crc32(name.encode()), seed]).standard_normal(out[name].shape)
        drawn = base * np.exp(spread * noise) if base else spread * noise
        out[name] = jnp.asarray(drawn.astype(out[name].dtype))
    for name, factor in factors.items():
        out[name] = (out[name] * factor).astype(out[name].dtype)
    return out
```

```python
from contextlib import ExitStack

import concourse.bass as bass
from concourse import mybir
import numpy as np

F32 = mybir.dt.float32
F32R = mybir.dt.float32r
I32 = mybir.dt.int32
ALU = mybir.AluOpType
ACT = mybir.ActivationFunctionType

P = 128
BATCH = 2048
DIM = 128
ROWS = [12500, 12500, 1250, 1250, 1250, 12500, 1000, 12500, 1250, 1000, 1250, 1250, 12500, 125000,
        1000, 1000, 12500, 1000, 1000, 1000, 12500, 1000, 1250, 1000, 12500, 1250]
TABLES = len(ROWS)
VECS = TABLES + 1
KPARTS = 8
HOT_ROWS = 1000
HOT_P = HOT_ROWS // KPARTS
HOT = [t for t, r in enumerate(ROWS) if r == HOT_ROWS][1:]
GATHERED = [t for t in range(TABLES) if t not in HOT]
NG, NH = len(GATHERED), len(HOT)
NE = NG + 1
ORDER = [0] + [1 + t for t in GATHERED] + [1 + t for t in HOT]

TILES = 2
CHUNK = TILES * P
CHUNKS = BATCH // CHUNK
GROUP = 4
GROUPS = P // GROUP
OTHER = VECS - 1
GP, GN = GROUP * VECS, GROUP * OTHER
GROUPS_BANK = 4
GBATCHES = GROUPS // GROUPS_BANK
TR_BANK = 4
TR_BATCHES = -(-NE // TR_BANK)
HALF = GROUPS // 2

WIN = OTHER // 2
ROW = VECS * OTHER
PAIRS = VECS * WIN
KT = 3
KP = PAIRS // KT
KWIN = VECS // KT
ZROW = ROW + WIN + DIM
H1, H2 = 512, 256
N1, N2 = H1 // P, H2 // P
M_USES = TILES + N1 + N2 + 1


def pair_rows():
    upper = {}
    for f in range(VECS):
        for g in range(f + 1, VECS):
            upper[f, g] = len(upper)
    rows = []
    for w in range(VECS):
        for j in range(WIN):
            at = (VECS * w + j) if w < VECS - 1 else WIN + j
            p, q = at // OTHER, at % OTHER + 1
            f, g = sorted((ORDER[p], ORDER[q]))
            rows.append(upper[f, g])
    assert sorted(rows) == list(range(len(upper)))
    return rows


def build(nc, dense, ids, ids_t, tables, w1_dense, w1_pairs, w1_last, b1, w2, b2, w3, y):
    ctx = ExitStack()
    with ctx:
        def sb(name, shape, dt=F32):
            return ctx.enter_context(nc.sbuf_tensor(name, shape, dt))

        def pb(name, shape):
            return ctx.enter_context(nc.psum_tensor(name, shape, F32))

        def sem(name):
            return ctx.enter_context(nc.semaphore(name))

        products_dram = nc.dram_tensor("products", (TILES, P, ROW), F32, kind="Internal").ap()

        tab_hi = sb("tab_hi", [P, NH, KPARTS, DIM], F32R)
        tab_lo = sb("tab_lo", [P, NH, KPARTS, DIM], F32R)
        row_of = sb("row_of", [P, KPARTS])
        row_of_i = sb("row_of_i", [P, KPARTS], I32)
        ident = sb("ident", [P, P])
        w1p = sb("w1p", [P, KT, H1])
        w1d = sb("w1d", [P, H1])
        w1e = sb("w1e", [P, H1])
        w2s = sb("w2s", [P, N1, H2])
        w3s = sb("w3s", [P, N2])
        b1s = sb("b1s", [P, N1])
        b2s = sb("b2s", [P, N2])
        idx_all = sb("idx_all", [P, CHUNKS * TILES * TABLES], I32)
        idx = sb("idx", [P, TILES, TABLES], I32)
        emb = sb("emb", [P, TILES, NE, DIM])
        vec = sb("vec", [P, CHUNK, VECS])
        hot_ids = sb("hot_ids", [P, NH, CHUNK], I32)
        onehot = sb("onehot", [P, 2, KPARTS, CHUNK], F32R)
        prod = sb("prod", [P, GROUPS, GN])
        zrow = sb("zrow", [P, TILES, ZROW])
        zpair = sb("zpair", [P, TILES, PAIRS])
        z = sb("z", [P, KT + 1, CHUNK])
        h1 = sb("h1", [P, N1, CHUNK])
        h2 = sb("h2", [P, N2, CHUNK])
        ys = sb("ys", [1, CHUNK])

        tr_ps = [pb(f"tr_ps{i}", [P, TR_BANK, P]) for i in range(2)]
        hot_ps = [pb(f"hot_ps{i}", [P, 2, CHUNK]) for i in range(2)]
        prod_ps = [pb(f"prod_ps{i}", [P, 512]) for i in range(2)]
        mlp_ps = [pb(f"mlp_ps{i}", [P, 512]) for i in range(2)]

        idx_in = sem("idx_in")
        idx_set = sem("idx_set")
        idx_known = sem("idx_known")
        zeroed = sem("zeroed")
        ident_set = sem("ident_set")
        numbered = sem("numbered")
        weights_in = sem("weights_in")
        tables_in = [sem(f"table{j}_in") for j in range(2)]
        w1d_set = sem("w1d_set")
        row_of_set = sem("row_of_set")
        hi_set = sem("hi_set")
        lo_set = sem("lo_set")
        dense_in = [sem(f"dense{i}_in") for i in range(TILES)]
        emb_in = [sem(f"emb{i}_in") for i in range(TILES)]
        emb_free = sem("emb_free")
        tr_ready = sem("tr_ready")
        tr_copied = sem("tr_copied")
        hot_ids_free = sem("hot_ids_free")
        hot_ids_in = sem("hot_ids_in")
        onehot_set = sem("onehot_set")
        looked_up = sem("looked_up")
        hot_copied = sem("hot_copied")
        prod_ready = sem("prod_ready")
        prod_copied = sem("prod_copied")
        prod_out = [sem(f"prod{h}_out") for h in range(2)]
        zrow_in = [sem(f"zrow{i}_in") for i in range(TILES)]
        pairs_packed = sem("pairs_packed")
        mlp_ready = sem("mlp_ready")
        mlp_copied = sem("mlp_copied")
        y_out = sem("y_out")

        WEIGHT_LOADS = 7

        def prod_stage(j):
            return prod[0:HOT_P, :, :].rearrange("p g n -> p (g n)")[
                :, j % 2 * KPARTS * DIM:(j % 2 + 1) * KPARTS * DIM]

        block = ctx.enter_context(nc.Block())

        @block.sync
        def _(sp):
            sp.dma_start(idx_all[:, :].rearrange("p (t f) -> p t f", f=TABLES),
                         ids.rearrange("(t p) f -> p t f", p=P)).then_inc(idx_in, 16)

            def load_dense(c, i):
                sp.dma_start(emb[:, i, 0, :], dense[bass.ds(c * CHUNK + i * P, P), :]
                             ).then_inc(dense_in[i], 16)

            def load_hot_ids(at):
                src = ids_t[:, bass.ds(at, CHUNK)]
                sp.dma_start(hot_ids[:, :, :], src.rearrange("(o f) b -> o f b", o=1)
                             .broadcast_to([P, NH, CHUNK])).then_inc(hot_ids_in, 16)

            def load_table(j):
                sp.dma_start(prod_stage(j), tables[HOT[j]].rearrange("(p k) d -> p (k d)", k=KPARTS)
                             ).then_inc(tables_in[j % 2], 16)

            load_hot_ids(0)
            load_dense(0, 0)
            load_dense(0, 1)
            for j in range(NH):
                if j >= 2:
                    sp.wait_ge(lo_set, j - 1)
                load_table(j)
            sp.dma_start(w1p[0:KP, :, :], w1_pairs.rearrange("(k p) n -> p k n", k=KT)).then_inc(weights_in, 16)
            sp.dma_start(w1d[:, :], w1_dense).then_inc(weights_in, 16)
            sp.dma_start(w1e[:, :], w1_last).then_inc(weights_in, 16)
            sp.dma_start(w2s[:, :, :], w2.rearrange("(k p) n -> p k n", k=N1)).then_inc(weights_in, 16)
            sp.dma_start(w3s[:, :], w3).then_inc(weights_in, 16)
            sp.dma_start(b1s[:, :], b1).then_inc(weights_in, 16)
            sp.dma_start(b2s[:, :], b2).then_inc(weights_in, 16)

            def store_products(c, i, h):
                sp.wait_ge(prod_copied, (c * TILES + i) * GBATCHES + (h + 1) * GBATCHES // 2)
                for s in range(GROUP):
                    dst = products_dram[i].rearrange("(t s) (v q) -> s v t q", s=GROUP, v=VECS)
                    sp.dma_start(dst[s, :, h * HALF:(h + 1) * HALF, :],
                                 prod[VECS * s:VECS * (s + 1), h * HALF:(h + 1) * HALF,
                                      s * OTHER:(s + 1) * OTHER]).then_inc(prod_out[h], 16)

            def load_rows(c, i):
                for h in range(2):
                    sp.wait_ge(prod_out[h], (c * TILES + i + 1) * GROUP * 16)
                sp.dma_start(zrow[:, i, 0:ROW], products_dram[i]).then_inc(zrow_in[i], 16)
                sp.dma_start(zrow[:, i, ROW:ROW + WIN], products_dram[i][:, WIN:2 * WIN]
                             ).then_inc(zrow_in[i], 16)
                sp.dma_start(zrow[:, i, ROW + WIN:ZROW], dense[bass.ds(c * CHUNK + i * P, P), :]
                             ).then_inc(zrow_in[i], 16)

            def chunk(c, last):
                if not last:
                    sp.wait_ge(tr_ready, (c * TILES + 1) * TR_BATCHES)
                    load_dense(c + 1, 0)
                    sp.wait_ge(onehot_set, (c + 1) * NH)
                    sp.sem_inc(hot_ids_free, 1)
                    load_hot_ids((c + 1) * CHUNK)
                    sp.wait_ge(tr_ready, (c * TILES + 2) * TR_BATCHES)
                    load_dense(c + 1, 1)
                store_products(c, 0, 0)
                store_products(c, 0, 1)
                store_products(c, 1, 0)
                load_rows(c, 0)
                store_products(c, 1, 1)
                load_rows(c, 1)

            with sp.Fori(0, CHUNKS - 1) as c:
                chunk(c, False)
            chunk(CHUNKS - 1, True)

        @block.gpsimd
        def _(pool):
            pool.iota(row_of_i[:, :], pattern=[[1, KPARTS]], base=0,
                      channel_multiplier=KPARTS).then_inc(numbered, 1)

            def gathers(c, first):
                for i in range(TILES):
                    if not first:
                        pool.wait_ge(tr_ready, ((c - 1) * TILES + i + 1) * TR_BATCHES)
                        pool.sem_inc(emb_free, 1)
                    at = (c * TILES + i) * TABLES
                    nc.gpsimd.tensor_copy(idx[:, i, :], idx_all[:, bass.ds(at, TABLES)]
                                          ).then_inc(idx_set, 1)
                    pool.wait_ge(idx_set, c * TILES + i + 1)
                    pool.sem_inc(idx_known, 1)
                    for n, t in enumerate(GATHERED):
                        nc.gpsimd.indirect_dma_start(
                            emb[:, i, 1 + n, :], None, tables[t],
                            bass.IndirectOffsetOnAxis(idx[:, i, t:t + 1], 0)).then_inc(emb_in[i], 16)

            def make_ident():
                nc.gpsimd.memset(ident[:, :], 0.0).then_inc(zeroed, 1)
                pool.wait_ge(zeroed, 1)
                nc.gpsimd.affine_select(out=ident[:, :], in_=ident[:, :], compare_op=ALU.not_equal,
                                        fill=1.0, base=0, pattern=[[-1, P]], channel_multiplier=1
                                        ).then_inc(ident_set, 1)

            make_ident()
            pool.wait_ge(idx_in, 16)
            gathers(0, True)
            with pool.Fori(1, CHUNKS) as c:
                gathers(c, False)

        @block.vector
        def _(dve):
            dve.wait_ge(numbered, 1)
            nc.vector.tensor_copy(row_of[:, :], row_of_i[:, :]).then_inc(row_of_set, 1)
            for j in range(NH):
                dve.wait_ge(hi_set, j + 1)
                nc.vector.tensor_tensor(
                    tab_lo[0:HOT_P, j, :, :].rearrange("p k d -> p (k d)"), prod_stage(j),
                    tab_hi[0:HOT_P, j, :, :].rearrange("p k d -> p (k d)"), ALU.subtract
                ).then_inc(lo_set, 1)
            dve.wait_ge(weights_in, WEIGHT_LOADS * 16)
            nc.vector.tensor_tensor(w1d[:, :], w1d[:, :], w1e[:, :], ALU.add).then_inc(w1d_set, 1)
            dve.wait_ge(row_of_set, 1)

            def copy_vectors(c, i):
                for k in range(TR_BATCHES):
                    n = min(TR_BANK, NE - k * TR_BANK)
                    dve.wait_ge(tr_ready, (c * TILES + i) * TR_BATCHES + k + 1)
                    nc.vector.tensor_copy(
                        vec[:, i * P:(i + 1) * P, k * TR_BANK:k * TR_BANK + n].rearrange("d b v -> d v b"),
                        tr_ps[(i * TR_BATCHES + k) % 2][:, 0:n, :]).then_inc(tr_copied, 1)

            def one_hots(c, which, first):
                for j in which:
                    if not (first and j < 2):
                        dve.wait_ge(looked_up, c * NH + j - 1)
                    for k in range(KPARTS):
                        last = nc.vector.tensor_scalar(
                            onehot[0:HOT_P, j % 2, k, :], hot_ids[0:HOT_P, j, :],
                            row_of[0:HOT_P, k:k + 1], None, ALU.is_equal)
                    last.then_inc(onehot_set, 1)

            def pack_pairs(c, i):
                dve.wait_ge(zrow_in[i], (c + 1) * 3 * 16)
                nc.vector.tensor_copy(
                    zpair[:, i, :].rearrange("b (w j) -> b w j", j=WIN),
                    zrow[:, i, 0:VECS * VECS].rearrange("b (w v) -> b w v", v=VECS)[:, :, 0:WIN]
                ).then_inc(pairs_packed, 1)

            copy_vectors(0, 0)
            dve.wait_ge(hot_ids_in, 16)
            one_hots(0, range(NH), True)
            copy_vectors(0, 1)
            with dve.Fori(1, CHUNKS) as c:
                copy_vectors(c, 0)
                pack_pairs(c - 1, 0)
                dve.wait_ge(hot_ids_in, (c + 1) * 16)
                one_hots(c, range(NH - 2), False)
                pack_pairs(c - 1, 1)
                one_hots(c, range(NH - 2, NH), False)
                copy_vectors(c, 1)
            for i in range(TILES):
                pack_pairs(CHUNKS - 1, i)

        @block.scalar
        def _(act):
            for j in range(NH):
                act.wait_ge(tables_in[j % 2], (j // 2 + 1) * 16)
                nc.scalar.activation(tab_hi[0:HOT_P, j, :, :].rearrange("p k d -> p (k d)"),
                                     prod_stage(j), ACT.Copy).then_inc(hi_set, 1)
            act.wait_ge(weights_in, WEIGHT_LOADS * 16)
            act.wait_ge(lo_set, NH)

            def copy_looked_up(c, q):
                act.wait_ge(looked_up, c * NH + 2 * q + 2)
                nc.scalar.activation(vec[:, :, NE + 2 * q:NE + 2 * q + 2].rearrange("d b v -> d v b"),
                                     hot_ps[q % 2][:, :, :], ACT.Copy).then_inc(hot_copied, 1)

            def copy_products(c, i, first):
                for k in range(GBATCHES):
                    if k % (GBATCHES // 2) == 0 and not (first and i == 0):
                        act.wait_ge(prod_out[k // (GBATCHES // 2)], (c * TILES + i) * GROUP * 16)
                    act.wait_ge(prod_ready, (c * TILES + i) * GBATCHES + k + 1)
                    nc.scalar.activation(
                        prod[0:GP, k * GROUPS_BANK:(k + 1) * GROUPS_BANK, :],
                        prod_ps[k % 2][0:GP, 0:GROUPS_BANK * GN].rearrange("p (g n) -> p g n", n=GN),
                        ACT.Copy).then_inc(prod_copied, 1)

            def mlp_use(c, u):
                act.wait_ge(mlp_ready, c * M_USES + u + 1)
                return mlp_ps[u % 2]

            def copy_pairs(c, i):
                ps = mlp_use(c, i)
                nc.scalar.activation(z[0:KP, 0:KT, i * P:(i + 1) * P],
                                     ps[0:KP, 0:KT * P].rearrange("p (k b) -> p k b", b=P), ACT.Copy)
                nc.scalar.activation(z[:, KT, i * P:(i + 1) * P], ps[:, KT * P:(KT + 1) * P],
                                     ACT.Copy).then_inc(mlp_copied, 1)

            def layer1(c):
                for n in range(N1):
                    ps = mlp_use(c, TILES + n)
                    nc.scalar.activation(h1[:, n, :], ps[:, 0:CHUNK], ACT.Relu,
                                         bias=b1s[:, n:n + 1]).then_inc(mlp_copied, 1)

            def layer2(c):
                for n in range(N2):
                    ps = mlp_use(c, TILES + N1 + n)
                    nc.scalar.activation(h2[:, n, :], ps[:, 0:CHUNK], ACT.Relu,
                                         bias=b2s[:, n:n + 1]).then_inc(mlp_copied, 1)

            def result(c, first):
                ps = mlp_use(c, M_USES - 1)
                if not first:
                    act.wait_ge(y_out, c * 16)
                nc.scalar.activation(ys[:, :], ps[0:1, 0:CHUNK], ACT.Copy).then_inc(mlp_copied, 1)
                act.wait_ge(mlp_copied, (c + 1) * M_USES)
                act.dma_start(y[:, bass.ds(c * CHUNK, CHUNK)], ys[:, :]).then_inc(y_out, 16)

            for q in range(NH // 2):
                copy_looked_up(0, q)
            copy_products(0, 0, True)
            copy_products(0, 1, True)

            def chunk(c, before, first):
                copy_pairs(before, 0)
                for q in range(NH // 2):
                    copy_looked_up(c, q)
                copy_pairs(before, 1)
                layer1(before)
                layer2(before)
                copy_products(c, 0, False)
                result(before, first)
                copy_products(c, 1, False)

            chunk(1, 0, True)
            with act.Fori(2, CHUNKS) as c:
                chunk(c, c - 1, False)
            last = CHUNKS - 1
            copy_pairs(last, 0)
            copy_pairs(last, 1)
            layer1(last)
            layer2(last)
            result(last, False)
            act.wait_ge(y_out, CHUNKS * 16)

        @block.tensor
        def _(pe):
            def transposes(c, i, first):
                pe.wait_ge(dense_in[i], (c + 1) * 16)
                pe.wait_ge(emb_in[i], (c + 1) * NG * 16)
                for k in range(TR_BATCHES):
                    m = i * TR_BATCHES + k
                    if not (first and m < 2):
                        pe.wait_ge(tr_copied, c * TILES * TR_BATCHES + m - 1)
                    for n in range(k * TR_BANK, min((k + 1) * TR_BANK, NE)):
                        last = nc.tensor.transpose(tr_ps[m % 2][:, n % TR_BANK, :], emb[:, i, n, :],
                                                   ident[:, :])
                    last.then_inc(tr_ready, 1)

            def look_up(c, first):
                for j in range(NH):
                    if j % 2 == 0 and not (first and j < 4):
                        pe.wait_ge(hot_copied, c * (NH // 2) + j // 2 - 1)
                    pe.wait_ge(onehot_set, c * NH + j + 1)
                    out = hot_ps[j // 2 % 2][:, j % 2, :]
                    for k in range(KPARTS):
                        for part, tab in enumerate((tab_hi, tab_lo)):
                            last = nc.tensor.matmul(out, tab[0:HOT_P, j, k, :],
                                                    onehot[0:HOT_P, j % 2, k, :],
                                                    start=(k == 0 and part == 0),
                                                    stop=(k == KPARTS - 1 and part == 1))
                    last.then_inc(looked_up, 1)

            def products(c, i, first):
                if i == 0:
                    pe.wait_ge(hot_copied, (c + 1) * (NH // 2))
                pe.wait_ge(tr_copied, (c * TILES + i + 1) * TR_BATCHES)
                for k in range(GBATCHES):
                    m = i * GBATCHES + k
                    if not (first and m < 2):
                        pe.wait_ge(prod_copied, c * TILES * GBATCHES + m - 1)
                    for g in range(GROUPS_BANK):
                        b = i * P + (k * GROUPS_BANK + g) * GROUP
                        last = nc.tensor.matmul(
                            prod_ps[k % 2][0:GP, g * GN:(g + 1) * GN],
                            vec[:, b:b + GROUP, :].rearrange("d b v -> d (b v)"),
                            vec[:, b:b + GROUP, 1:VECS], start=True, stop=True)
                    last.then_inc(prod_ready, 1)

            def mlp_bank(c, u, first):
                if u >= 2:
                    pe.wait_ge(mlp_copied, c * M_USES + u - 1)
                elif not first:
                    pe.wait_ge(mlp_copied, c * M_USES)
                return mlp_ps[u % 2]

            def pairs(c, i, first):
                pe.wait_ge(pairs_packed, c * TILES + i + 1)
                ps = mlp_bank(c, i, first)
                for k in range(KT):
                    nc.tensor.transpose(ps[0:KP, k * P:(k + 1) * P], zpair[:, i, k * KP:(k + 1) * KP],
                                        ident[:, :])
                nc.tensor.transpose(ps[:, KT * P:(KT + 1) * P], zrow[:, i, ROW + WIN:ZROW],
                                    ident[:, :]).then_inc(mlp_ready, 1)

            def layer1(c, first):
                pe.wait_ge(mlp_copied, c * M_USES + TILES)
                for n in range(N1):
                    ps = mlp_bank(c, TILES + n, first)
                    for k in range(KT + 1):
                        rows = KP if k < KT else P
                        w = w1p[0:KP, k, n * P:(n + 1) * P] if k < KT else w1d[:, n * P:(n + 1) * P]
                        last = nc.tensor.matmul(ps[:, 0:CHUNK], w, z[0:rows, k, :],
                                                start=(k == 0), stop=(k == KT))
                    last.then_inc(mlp_ready, 1)

            def layer2(c, first):
                pe.wait_ge(mlp_copied, c * M_USES + TILES + N1)
                for n in range(N2):
                    ps = mlp_bank(c, TILES + N1 + n, first)
                    for k in range(N1):
                        last = nc.tensor.matmul(ps[:, 0:CHUNK], w2s[:, k, n * P:(n + 1) * P], h1[:, k, :],
                                                start=(k == 0), stop=(k == N1 - 1))
                    last.then_inc(mlp_ready, 1)

            def layer3(c, first):
                pe.wait_ge(mlp_copied, c * M_USES + TILES + N1 + N2)
                ps = mlp_bank(c, M_USES - 1, first)
                for k in range(N2):
                    last = nc.tensor.matmul(ps[0:1, 0:CHUNK], w3s[:, k:k + 1], h2[:, k, :],
                                            start=(k == 0), stop=(k == N2 - 1))
                last.then_inc(mlp_ready, 1)

            pe.wait_ge(ident_set, 1)
            pe.wait_ge(w1d_set, 1)
            transposes(0, 0, True)
            look_up(0, True)
            transposes(0, 1, True)
            products(0, 0, True)
            products(0, 1, True)

            def chunk(c, before, first):
                transposes(c, 0, False)
                pairs(before, 0, first)
                look_up(c, False)
                pairs(before, 1, first)
                layer1(before, first)
                transposes(c, 1, False)
                layer2(before, first)
                products(c, 0, False)
                layer3(before, first)
                products(c, 1, False)

            chunk(1, 0, True)
            with pe.Fori(2, CHUNKS) as c:
                chunk(c, c - 1, False)
            last = CHUNKS - 1
            pairs(last, 0, False)
            pairs(last, 1, False)
            layer1(last, False)
            layer2(last, False)
            layer3(last, False)


def kernel(**inputs):
    import concourse.bacc as _bacc
    from concourse.bass_utils import run_bass_kernel_spmd as _run

    w1 = np.asarray(inputs["W_top1"])
    ids = np.asarray(inputs["ids"])
    arrays = {
        "dense": np.asarray(inputs["r_dense_features"]),
        "ids": ids,
        "ids_t": ids[:, HOT].T,
        "w1_dense": w1[:DIM],
        "w1_pairs": w1[DIM:DIM + PAIRS][pair_rows()],
        "w1_last": w1[DIM + PAIRS:],
        "b1": np.asarray(inputs["b_top1"]).reshape(N1, P).T,
        "w2": np.asarray(inputs["W_top2"]),
        "b2": np.asarray(inputs["b_top2"]).reshape(N2, P).T,
        "w3": np.asarray(inputs["W_top3"]).reshape(N2, P).T,
    }
    arrays |= {f"tbl_{t}": np.asarray(inputs[f"tbl_{t}"]) for t in range(TABLES)}
    arrays = {k: np.ascontiguousarray(a) for k, a in arrays.items()}

    nc = _bacc.Bacc("TRN2", target_bir_lowering=False, num_devices=1)
    ap = {k: nc.dram_tensor(f"in_{k}", a.shape, mybir.dt.from_np(a.dtype), kind="ExternalInput").ap()
          for k, a in arrays.items()}
    y = nc.dram_tensor("y", (1, BATCH), F32, kind="ExternalOutput").ap()
    build(nc, ap["dense"], ap["ids"], ap["ids_t"], [ap[f"tbl_{t}"] for t in range(TABLES)],
          ap["w1_dense"], ap["w1_pairs"], ap["w1_last"], ap["b1"], ap["w2"], ap["b2"], ap["w3"], y)
    r = _run(nc, [{f"in_{k}": a for k, a in arrays.items()}], core_ids=[0])
    return r.results[0]["y"].reshape(BATCH, 1)
```

```python
from contextlib import ExitStack

import concourse.bass as bass
from concourse import mybir
import numpy as np

F32 = mybir.dt.float32
F32R = mybir.dt.float32r
I32 = mybir.dt.int32
ALU = mybir.AluOpType
ACT = mybir.ActivationFunctionType

P = 128
BATCH = 2048
DIM = 128
ROWS = [12500, 12500, 1250, 1250, 1250, 12500, 1000, 12500, 1250, 1000, 1250, 1250, 12500, 125000,
        1000, 1000, 12500, 1000, 1000, 1000, 12500, 1000, 1250, 1000, 12500, 1250]
TABLES = len(ROWS)
VECS = TABLES + 1
UNIT = 2
KPARTS = 8
HOT_ROWS = 1000
HOT_P = HOT_ROWS // KPARTS
HOT = [t for t, r in enumerate(ROWS) if r == HOT_ROWS][1:]
GATHERED = [t for t in range(TABLES) if t not in HOT]
NG, NH = len(GATHERED), len(HOT)
NE = NG + 1
ORDER = [0] + [1 + t for t in GATHERED] + [1 + t for t in HOT]

TILES = 2
CHUNK = TILES * P
CHUNKS = BATCH // CHUNK
GROUP = 4
GROUPS = P // GROUP
OTHER = VECS - 1
GP, GN = GROUP * VECS, GROUP * OTHER
GROUPS_BANK = 4
BANKS = 4
GBATCHES = GROUPS // GROUPS_BANK
TR_BANK = 4
TR_BATCHES = -(-NE // TR_BANK)
HALF = GROUPS // 2
UNITS = NH * KPARTS // UNIT
RING = KPARTS // UNIT
STAGES = 3

WIN = OTHER // 2
ROW = VECS * OTHER
PAIRS = VECS * WIN
KT = 3
KP = PAIRS // KT
KWIN = VECS // KT
ZROW = ROW + WIN + DIM
H1, H2 = 512, 256
N1, N2 = H1 // P, H2 // P
M_USES = TILES + N1 + N2 + 1


def pair_rows():
    upper = {}
    for f in range(VECS):
        for g in range(f + 1, VECS):
            upper[f, g] = len(upper)
    rows = []
    for w in range(VECS):
        for j in range(WIN):
            at = (VECS * w + j) if w < VECS - 1 else WIN + j
            p, q = at // OTHER, at % OTHER + 1
            f, g = sorted((ORDER[p], ORDER[q]))
            rows.append(upper[f, g])
    assert sorted(rows) == list(range(len(upper)))
    return rows


def build(nc, dense, ids, ids_t, tables, w1_dense, w1_pairs, w1_last, b1, w2, b2, w3, y):
    ctx = ExitStack()
    with ctx:
        def sb(name, shape, dt=F32):
            return ctx.enter_context(nc.sbuf_tensor(name, shape, dt))

        def pb(name, shape):
            return ctx.enter_context(nc.psum_tensor(name, shape, F32))

        def sem(name):
            return ctx.enter_context(nc.semaphore(name))

        products_dram = nc.dram_tensor("products", (TILES, P, ROW), F32, kind="Internal").ap()

        tab_hi = sb("tab_hi", [P, NH, KPARTS, DIM], F32R)
        tab_lo = sb("tab_lo", [P, NH, KPARTS, DIM], F32R)
        row_of = sb("row_of", [P, KPARTS])
        row_of_i = sb("row_of_i", [P, KPARTS], I32)
        ident = sb("ident", [P, P])
        w1p = [sb(f"w1p_{x}", [P, KT, H1], F32R) for x in ("high", "low")]
        w1d = [sb(f"w1d_{x}", [P, H1], F32R) for x in ("high", "low")]
        w2s = [sb(f"w2_{x}", [P, N1, H2], F32R) for x in ("high", "low")]
        w3s = sb("w3s", [P, N2])
        b1s = sb("b1s", [P, N1])
        b2s = sb("b2s", [P, N2])
        idx = sb("idx", [P, TILES, TABLES], I32)
        emb = sb("emb", [P, TILES, NE, DIM])
        vec = sb("vec", [P, CHUNK, VECS])
        hot_ids = sb("hot_ids", [P, NH, CHUNK], I32)
        onehot = sb("onehot", [P, 2, KPARTS, CHUNK], F32R)
        prod = sb("prod", [P, GROUPS, GN])
        zrow = sb("zrow", [P, TILES, ZROW])
        zpair = sb("zpair", [P, TILES, PAIRS])
        z = [sb(f"z_{x}", [P, KT + 1, CHUNK], F32R) for x in ("high", "low")]
        h1 = sb("h1", [P, N1, CHUNK])
        h1s = [sb(f"h1_{x}", [P, N1, CHUNK], F32R) for x in ("high", "low")]
        h2 = sb("h2", [P, N2, CHUNK])
        ys = sb("ys", [1, CHUNK])
        w1p_in = zrow[0:KP, :, :].rearrange("p i r -> p (i r)")[:, 0:KT * H1].rearrange(
            "p (k n) -> p k n", n=H1)
        w1d_in = zpair[:, :, :].rearrange("p i r -> p (i r)")[:, 0:H1]
        w1e_in = h2[:, :, :].rearrange("p n b -> p (n b)")
        w2_in = h1[:, :, :]

        bank_ps = [pb(f"bank_ps{i}", [P, 512]) for i in range(BANKS)]
        hot_ps = [pb(f"hot_ps{i}", [P, 2, CHUNK]) for i in range(2)]
        mlp_ps = [pb(f"mlp_ps{i}", [P, 512]) for i in range(2)]

        idx_in = [sem(f"idx{i}_in") for i in range(TILES)]
        idx_known = sem("idx_known")
        zeroed = sem("zeroed")
        ident_set = sem("ident_set")
        numbered = sem("numbered")
        weights_in = sem("weights_in")
        tables_in = [sem(f"table{j}_in") for j in range(STAGES)]
        weights_added = sem("weights_added")
        weights_high = sem("weights_high")
        weights_low = sem("weights_low")
        row_of_set = sem("row_of_set")
        hi_set = sem("hi_set")
        lo_set = sem("lo_set")
        dense_in = [sem(f"dense{i}_in") for i in range(TILES)]
        emb_in = [sem(f"emb{i}_in") for i in range(TILES)]
        emb_free = sem("emb_free")
        tr_ready = sem("tr_ready")
        tr_copied = sem("tr_copied")
        hot_ids_free = sem("hot_ids_free")
        hot_ids_in = sem("hot_ids_in")
        onehot_set = sem("onehot_set")
        looked_up = sem("looked_up")
        hot_copied = sem("hot_copied")
        prod_ready = sem("prod_ready")
        prod_copied = sem("prod_copied")
        prod_out = [sem(f"prod{h}_out") for h in range(2)]
        zrow_in = [sem(f"zrow{i}_in") for i in range(TILES)]
        z_high = sem("z_high")
        z_low = sem("z_low")
        h1_high = sem("h1_high")
        h1_low = sem("h1_low")
        pairs_packed = sem("pairs_packed")
        mlp_ready = sem("mlp_ready")
        mlp_copied = sem("mlp_copied")
        y_out = sem("y_out")

        WEIGHT_LOADS = 7

        def prod_stage(j):
            return prod[0:HOT_P, :, :].rearrange("p g n -> p (g n)")[
                :, j % STAGES * KPARTS * DIM:(j % STAGES + 1) * KPARTS * DIM]

        block = ctx.enter_context(nc.Block())

        @block.sync
        def _(sp):
            def load_indices(c, i):
                sp.dma_start(idx[:, i, :], ids[bass.ds(c * CHUNK + i * P, P), :]
                             ).then_inc(idx_in[i], 16)

            def load_dense(c, i):
                sp.dma_start(emb[:, i, 0, :], dense[bass.ds(c * CHUNK + i * P, P), :]
                             ).then_inc(dense_in[i], 16)

            def load_hot_ids(at):
                src = ids_t[:, bass.ds(at, CHUNK)]
                sp.dma_start(hot_ids[:, :, :], src.rearrange("(o f) b -> o f b", o=1)
                             .broadcast_to([P, NH, CHUNK])).then_inc(hot_ids_in, 16)

            def load_table(j):
                src = tables[HOT[j]].rearrange("(p k) d -> p (k d)", k=KPARTS)
                for a, b in ((0, HOT_P // 16 * 16), (HOT_P // 16 * 16, HOT_P)):
                    sp.dma_start(prod_stage(j)[a:b, :], src[a:b, :]).then_inc(tables_in[j % STAGES], 16)

            load_indices(0, 0)
            load_table(0)
            load_hot_ids(0)
            load_indices(0, 1)
            load_table(1)
            load_table(2)
            load_dense(0, 0)
            load_dense(0, 1)
            for j in range(STAGES, NH):
                sp.wait_ge(lo_set, j - STAGES + 1)
                load_table(j)
            sp.dma_start(w1p_in, w1_pairs.rearrange("(k p) n -> p k n", k=KT)).then_inc(weights_in, 16)
            sp.dma_start(w1d_in, w1_dense).then_inc(weights_in, 16)
            sp.dma_start(w1e_in, w1_last).then_inc(weights_in, 16)
            sp.dma_start(w2_in, w2.rearrange("(k p) n -> p k n", k=N1)).then_inc(weights_in, 16)
            sp.dma_start(w3s[:, :], w3).then_inc(weights_in, 16)
            sp.dma_start(b1s[:, :], b1).then_inc(weights_in, 16)
            sp.dma_start(b2s[:, :], b2).then_inc(weights_in, 16)
            sp.wait_ge(weights_low, 3)

            def store_products(c, i, h):
                sp.wait_ge(prod_copied, (c * TILES + i) * GBATCHES + (h + 1) * GBATCHES // 2)
                for s in range(GROUP):
                    dst = products_dram[i].rearrange("(t s) (v q) -> s v t q", s=GROUP, v=VECS)
                    sp.dma_start(dst[s, :, h * HALF:(h + 1) * HALF, :],
                                 prod[VECS * s:VECS * (s + 1), h * HALF:(h + 1) * HALF,
                                      s * OTHER:(s + 1) * OTHER]).then_inc(prod_out[h], 16)

            def load_rows(c, i):
                for h in range(2):
                    sp.wait_ge(prod_out[h], (c * TILES + i + 1) * GROUP * 16)
                sp.dma_start(zrow[:, i, 0:ROW], products_dram[i]).then_inc(zrow_in[i], 16)
                sp.dma_start(zrow[:, i, ROW:ROW + WIN], products_dram[i][:, WIN:2 * WIN]
                             ).then_inc(zrow_in[i], 16)
                sp.dma_start(zrow[:, i, ROW + WIN:ZROW], dense[bass.ds(c * CHUNK + i * P, P), :]
                             ).then_inc(zrow_in[i], 16)

            def store_result(c):
                sp.wait_ge(mlp_copied, (c + 1) * (N2 + 1))
                sp.dma_start(y[:, bass.ds(c * CHUNK, CHUNK)], ys[:, :]).then_inc(y_out, 16)

            def chunk(c, first=False, to_load=2):
                if to_load:
                    sp.wait_ge(emb_in[1], (c + 1) * NG * 16)
                    load_indices(c + 1, 1)
                    sp.wait_ge(tr_ready, (c * TILES + 1) * TR_BATCHES)
                    load_dense(c + 1, 0)
                    sp.wait_ge(onehot_set, (c + 1) * UNITS)
                    sp.sem_inc(hot_ids_free, 1)
                    load_hot_ids((c + 1) * CHUNK)
                    sp.wait_ge(tr_ready, (c * TILES + 2) * TR_BATCHES)
                    load_dense(c + 1, 1)
                store_products(c, 0, 0)
                store_products(c, 0, 1)
                if to_load > 1:
                    sp.wait_ge(emb_in[0], (c + 2) * NG * 16)
                    load_indices(c + 2, 0)
                store_products(c, 1, 0)
                load_rows(c, 0)
                store_products(c, 1, 1)
                load_rows(c, 1)
                if not first:
                    store_result(c - 1)

            sp.wait_ge(emb_in[0], NG * 16)
            load_indices(1, 0)
            chunk(0, first=True)
            with sp.Fori(1, CHUNKS - 2) as c:
                chunk(c)
            chunk(CHUNKS - 2, to_load=1)
            chunk(CHUNKS - 1, to_load=0)
            store_result(CHUNKS - 1)
            sp.wait_ge(y_out, CHUNKS * 16)

        @block.gpsimd
        def _(pool):
            pool.iota(row_of_i[:, :], pattern=[[1, KPARTS]], base=0,
                      channel_multiplier=KPARTS).then_inc(numbered, 1)

            def gathers(c, first):
                for i in range(TILES):
                    if not first:
                        pool.wait_ge(tr_ready, ((c - 1) * TILES + i + 1) * TR_BATCHES)
                        pool.sem_inc(emb_free, 1)
                    pool.wait_ge(idx_in[i], (c + 1) * 16)
                    pool.sem_inc(idx_known, 1)
                    for n, t in enumerate(GATHERED):
                        nc.gpsimd.indirect_dma_start(
                            emb[:, i, 1 + n, :], None, tables[t],
                            bass.IndirectOffsetOnAxis(idx[:, i, t:t + 1], 0)).then_inc(emb_in[i], 16)

            def make_ident():
                nc.gpsimd.memset(ident[:, :], 0.0).then_inc(zeroed, 1)
                pool.wait_ge(zeroed, 1)
                nc.gpsimd.affine_select(out=ident[:, :], in_=ident[:, :], compare_op=ALU.not_equal,
                                        fill=1.0, base=0, pattern=[[-1, P]], channel_multiplier=1
                                        ).then_inc(ident_set, 1)

            make_ident()
            gathers(0, True)
            with pool.Fori(1, CHUNKS) as c:
                gathers(c, False)

        @block.vector
        def _(dve):
            dve.wait_ge(numbered, 1)
            nc.vector.tensor_copy(row_of[:, :], row_of_i[:, :]).then_inc(row_of_set, 1)
            dve.wait_ge(row_of_set, 1)

            def low_table(j):
                dve.wait_ge(hi_set, j + 1)
                nc.vector.tensor_tensor(
                    tab_lo[0:HOT_P, j, :, :].rearrange("p k d -> p (k d)"), prod_stage(j),
                    tab_hi[0:HOT_P, j, :, :].rearrange("p k d -> p (k d)"), ALU.subtract
                ).then_inc(lo_set, 1)

            def low_weights():
                dve.wait_ge(weights_in, WEIGHT_LOADS * 16)
                nc.vector.tensor_tensor(w1d_in, w1d_in, w1e_in, ALU.add).then_inc(weights_added, 1)
                dve.wait_ge(weights_high, 3)
                nc.vector.tensor_tensor(w1p[1][0:KP, :, :], w1p_in, w1p[0][0:KP, :, :], ALU.subtract
                                        ).then_inc(weights_low, 1)
                nc.vector.tensor_tensor(w1d[1][:, :], w1d_in, w1d[0][:, :], ALU.subtract
                                        ).then_inc(weights_low, 1)
                nc.vector.tensor_tensor(w2s[1][:, :, :], w2_in, w2s[0][:, :, :], ALU.subtract
                                        ).then_inc(weights_low, 1)

            def one_hots(c, j, first=False):
                for u in range(RING):
                    if not (first and j < 2):
                        dve.wait_ge(looked_up, c * UNITS + (j - 2) * RING + u + 1)
                    for k in range(u * UNIT, (u + 1) * UNIT):
                        last = nc.vector.tensor_scalar(
                            onehot[0:HOT_P, j % 2, k, :], hot_ids[0:HOT_P, j, :],
                            row_of[0:HOT_P, k:k + 1], None, ALU.is_equal)
                    last.then_inc(onehot_set, 1)

            def pack_pairs(c, i):
                dve.wait_ge(zrow_in[i], (c + 1) * 3 * 16)
                nc.vector.tensor_copy(
                    zpair[:, i, :].rearrange("b (w j) -> b w j", j=WIN),
                    zrow[:, i, 0:VECS * VECS].rearrange("b (w v) -> b w v", v=VECS)[:, :, 0:WIN]
                ).then_inc(pairs_packed, 1)

            def low_pairs(c, i):
                dve.wait_ge(z_high, c * TILES + i + 1)
                at = slice(i * P, (i + 1) * P)
                nc.vector.tensor_tensor(
                    z[1][0:KP, 0:KT, at], mlp_ps[i % 2][0:KP, 0:KT * P].rearrange("p (k b) -> p k b", b=P),
                    z[0][0:KP, 0:KT, at], ALU.subtract).then_inc(z_low, 1)
                nc.vector.tensor_tensor(
                    z[1][:, KT, at], mlp_ps[i % 2][:, KT * P:(KT + 1) * P], z[0][:, KT, at],
                    ALU.subtract).then_inc(z_low, 1)

            def low_h1(c, n):
                dve.wait_ge(h1_high, c * N1 + n + 1)
                nc.vector.tensor_tensor(h1s[1][:, n, :], h1[:, n, :], h1s[0][:, n, :], ALU.subtract
                                        ).then_inc(h1_low, 1)

            dve.wait_ge(hot_ids_in, 16)
            for j in range(NH):
                low_table(j)
                one_hots(0, j, True)
            low_weights()

            def chunk(c):
                before = c - 1
                dve.wait_ge(hot_ids_in, (c + 1) * 16)
                for j in range(4):
                    one_hots(c, j)
                pack_pairs(before, 0)
                one_hots(c, 4)
                pack_pairs(before, 1)
                one_hots(c, 5)
                low_pairs(before, 0)
                one_hots(c, 6)
                low_pairs(before, 1)
                one_hots(c, 7)
                for n in range(N1):
                    low_h1(before, n)

            with dve.Fori(1, CHUNKS) as c:
                chunk(c)
            last = CHUNKS - 1
            for i in range(TILES):
                pack_pairs(last, i)
                low_pairs(last, i)
            for n in range(N1):
                low_h1(last, n)

        @block.scalar
        def _(act):
            def high_table(j):
                act.wait_ge(tables_in[j % STAGES], (j // STAGES + 1) * 2 * 16)
                nc.scalar.activation(tab_hi[0:HOT_P, j, :, :].rearrange("p k d -> p (k d)"),
                                     prod_stage(j), ACT.Copy).then_inc(hi_set, 1)

            def copy_vectors(c, i, banks):
                for k in banks:
                    n = min(TR_BANK, NE - k * TR_BANK)
                    act.wait_ge(tr_ready, (c * TILES + i) * TR_BATCHES + k + 1)
                    nc.scalar.activation(
                        vec[:, i * P:(i + 1) * P, k * TR_BANK:k * TR_BANK + n].rearrange("d b v -> d v b"),
                        bank_ps[k % BANKS][:, 0:n * P].rearrange("d (v b) -> d v b", b=P), ACT.Copy
                    ).then_inc(tr_copied, 1)

            def copy_looked_up(c, q):
                act.wait_ge(looked_up, c * UNITS + 2 * (q + 1) * RING)
                nc.scalar.activation(vec[:, :, NE + 2 * q:NE + 2 * q + 2].rearrange("d b v -> d v b"),
                                     hot_ps[q % 2][:, :, :], ACT.Copy).then_inc(hot_copied, 1)

            def high_weights():
                act.wait_ge(weights_in, WEIGHT_LOADS * 16)
                nc.scalar.activation(w1p[0][0:KP, :, :], w1p_in, ACT.Copy).then_inc(weights_high, 1)
                nc.scalar.activation(w2s[0][:, :, :], w2_in, ACT.Copy).then_inc(weights_high, 1)
                act.wait_ge(weights_added, 1)
                nc.scalar.activation(w1d[0][:, :], w1d_in, ACT.Copy).then_inc(weights_high, 1)

            def copy_products(c, i, first):
                for k in range(GBATCHES):
                    if k % (GBATCHES // 2) == 0 and not (first and i == 0):
                        act.wait_ge(prod_out[k // (GBATCHES // 2)], (c * TILES + i) * GROUP * 16)
                    act.wait_ge(prod_ready, (c * TILES + i) * GBATCHES + k + 1)
                    nc.scalar.activation(
                        prod[0:GP, k * GROUPS_BANK:(k + 1) * GROUPS_BANK, :],
                        bank_ps[k % BANKS][0:GP, 0:GROUPS_BANK * GN].rearrange(
                            "p (g n) -> p g n", n=GN),
                        ACT.Copy).then_inc(prod_copied, 1)

            def mlp_use(c, u):
                act.wait_ge(mlp_ready, c * M_USES + u + 1)
                return mlp_ps[u % 2]

            def high_pairs(c, i):
                ps = mlp_use(c, i)
                nc.scalar.activation(z[0][0:KP, 0:KT, i * P:(i + 1) * P],
                                     ps[0:KP, 0:KT * P].rearrange("p (k b) -> p k b", b=P), ACT.Copy)
                nc.scalar.activation(z[0][:, KT, i * P:(i + 1) * P], ps[:, KT * P:(KT + 1) * P],
                                     ACT.Copy).then_inc(z_high, 1)

            def layer1(c, n):
                ps = mlp_use(c, TILES + n)
                nc.scalar.activation(h1[:, n, :], ps[:, 0:CHUNK], ACT.Relu, bias=b1s[:, n:n + 1])
                nc.scalar.activation(h1s[0][:, n, :], ps[:, 0:CHUNK], ACT.Relu, bias=b1s[:, n:n + 1]
                                     ).then_inc(h1_high, 1)

            def layer2(c, n):
                ps = mlp_use(c, TILES + N1 + n)
                nc.scalar.activation(h2[:, n, :], ps[:, 0:CHUNK], ACT.Relu,
                                     bias=b2s[:, n:n + 1]).then_inc(mlp_copied, 1)

            def result(c, first):
                ps = mlp_use(c, M_USES - 1)
                if not first:
                    act.wait_ge(y_out, c * 16)
                nc.scalar.activation(ys[:, :], ps[0:1, 0:CHUNK], ACT.Copy).then_inc(mlp_copied, 1)

            for j in range(2):
                high_table(j)
            for q in range(NH // 2):
                for j in range(2 * q + 2, min(2 * q + 4, NH)):
                    high_table(j)
                copy_looked_up(0, q)
            copy_vectors(0, 0, range(TR_BATCHES))
            high_weights()
            copy_vectors(0, 1, range(TR_BATCHES))
            act.wait_ge(lo_set, NH)
            copy_products(0, 0, True)
            copy_products(0, 1, True)
            act.wait_ge(weights_low, 3)

            def chunk(c, before, first):
                copy_vectors(c, 0, range(TR_BATCHES))
                copy_looked_up(c, 0)
                copy_looked_up(c, 1)
                high_pairs(before, 0)
                copy_looked_up(c, 2)
                high_pairs(before, 1)
                layer1(before, 0)
                copy_looked_up(c, 3)
                copy_vectors(c, 1, range(TR_BATCHES))
                layer1(before, 1)
                layer1(before, 2)
                layer1(before, 3)
                copy_products(c, 0, False)
                layer2(before, 0)
                layer2(before, 1)
                copy_products(c, 1, False)
                result(before, first)

            chunk(1, 0, True)
            with act.Fori(2, CHUNKS) as c:
                chunk(c, c - 1, False)
            last = CHUNKS - 1
            for i in range(TILES):
                high_pairs(last, i)
            for n in range(N1):
                layer1(last, n)
            layer2(last, 0)
            layer2(last, 1)
            result(last, False)

        @block.tensor
        def _(pe):
            def transposes(c, i, banks, first=False):
                if banks[0] == 0:
                    pe.wait_ge(dense_in[i], (c + 1) * 16)
                    pe.wait_ge(emb_in[i], (c + 1) * NG * 16)
                for k in banks:
                    if k >= BANKS:
                        pe.wait_ge(tr_copied, (c * TILES + i) * TR_BATCHES + k - BANKS + 1)
                    elif i > 0:
                        before = k + (TR_BATCHES - 1 - k) // BANKS * BANKS
                        pe.wait_ge(tr_copied, (c * TILES + i - 1) * TR_BATCHES + before + 1)
                    elif not first:
                        pe.wait_ge(prod_copied, c * TILES * GBATCHES - BANKS + k + 1)
                    for n in range(k * TR_BANK, min((k + 1) * TR_BANK, NE)):
                        at = n % TR_BANK * P
                        last = nc.tensor.transpose(bank_ps[k % BANKS][:, at:at + P], emb[:, i, n, :],
                                                   ident[:, :])
                    last.then_inc(tr_ready, 1)

            def look_up(c, j, first=False):
                if first:
                    pe.wait_ge(lo_set, j + 1)
                if j % 2 == 0 and not (first and j < 4):
                    pe.wait_ge(hot_copied, c * (NH // 2) + j // 2 - 1)
                out = hot_ps[j // 2 % 2][:, j % 2, :]
                for k in range(KPARTS):
                    if k % UNIT == 0:
                        pe.wait_ge(onehot_set, c * UNITS + j * RING + k // UNIT + 1)
                    for part, tab in enumerate((tab_hi, tab_lo)):
                        last = nc.tensor.matmul(out, tab[0:HOT_P, j, k, :], onehot[0:HOT_P, j % 2, k, :],
                                                start=(k == 0 and part == 0),
                                                stop=(k == KPARTS - 1 and part == 1))
                    if k % UNIT == UNIT - 1:
                        last.then_inc(looked_up, 1)

            def products(c, i, first=False):
                if i == 0:
                    pe.wait_ge(hot_copied, (c + 1) * (NH // 2))
                if i == 0:
                    pe.wait_ge(tr_copied, (c + 1) * TILES * TR_BATCHES)
                for k in range(GBATCHES):
                    m = i * GBATCHES + k
                    if m >= BANKS:
                        pe.wait_ge(prod_copied, c * TILES * GBATCHES + m - BANKS + 1)
                    for g in range(GROUPS_BANK):
                        b = i * P + (k * GROUPS_BANK + g) * GROUP
                        last = nc.tensor.matmul(
                            bank_ps[k % BANKS][0:GP, g * GN:(g + 1) * GN],
                            vec[:, b:b + GROUP, :].rearrange("d b v -> d (b v)"),
                            vec[:, b:b + GROUP, 1:VECS], start=True, stop=True)
                    last.then_inc(prod_ready, 1)

            def mlp_bank(c, u, first):
                if u < TILES:
                    if not first:
                        pe.wait_ge(mlp_copied, c * (N2 + 1))
                elif u < 2 * TILES:
                    pe.wait_ge(z_low, c * TILES * 2 + 2 * (u - TILES) + 2)
                elif u < TILES + N1 + 2:
                    pe.wait_ge(h1_high, c * N1 + u - TILES - 1)
                else:
                    pe.wait_ge(mlp_copied, c * (N2 + 1) + u - TILES - N1 - 1)
                return mlp_ps[u % 2]

            def pairs(c, i, first):
                pe.wait_ge(pairs_packed, c * TILES + i + 1)
                ps = mlp_bank(c, i, first)
                for k in range(KT):
                    nc.tensor.transpose(ps[0:KP, k * P:(k + 1) * P], zpair[:, i, k * KP:(k + 1) * KP],
                                        ident[:, :])
                nc.tensor.transpose(ps[:, KT * P:(KT + 1) * P], zrow[:, i, ROW + WIN:ZROW],
                                    ident[:, :]).then_inc(mlp_ready, 1)

            TERMS = ((0, 0), (0, 1), (1, 0))

            def layer1(c, n, first):
                pe.wait_ge(z_low, (c + 1) * TILES * 2)
                ps = mlp_bank(c, TILES + n, first)
                for k in range(KT + 1):
                    rows = KP if k < KT else P
                    for a, b in TERMS:
                        w = (w1p[a][0:KP, k, n * P:(n + 1) * P] if k < KT else
                             w1d[a][:, n * P:(n + 1) * P])
                        last = nc.tensor.matmul(ps[:, 0:CHUNK], w, z[b][0:rows, k, :],
                                                start=(k == 0 and a + b == 0),
                                                stop=(k == KT and a == 1))
                last.then_inc(mlp_ready, 1)

            def layer2(c, n, first):
                pe.wait_ge(h1_low, (c + 1) * N1)
                ps = mlp_bank(c, TILES + N1 + n, first)
                for k in range(N1):
                    for a, b in TERMS:
                        last = nc.tensor.matmul(ps[:, 0:CHUNK], w2s[a][:, k, n * P:(n + 1) * P],
                                                h1s[b][:, k, :], start=(k == 0 and a + b == 0),
                                                stop=(k == N1 - 1 and a == 1))
                last.then_inc(mlp_ready, 1)

            def layer3(c, first):
                pe.wait_ge(mlp_copied, c * (N2 + 1) + N2)
                ps = mlp_bank(c, M_USES - 1, first)
                for k in range(N2):
                    last = nc.tensor.matmul(ps[0:1, 0:CHUNK], w3s[:, k:k + 1], h2[:, k, :],
                                            start=(k == 0), stop=(k == N2 - 1))
                last.then_inc(mlp_ready, 1)

            for j in range(NH):
                look_up(0, j, True)
            pe.wait_ge(ident_set, 1)
            transposes(0, 0, range(TR_BATCHES), True)
            transposes(0, 1, range(TR_BATCHES), True)
            products(0, 0, True)
            products(0, 1, True)
            pe.wait_ge(weights_low, 3)

            def chunk(c, before, first):
                transposes(c, 0, range(TR_BATCHES))
                look_up(c, 0)
                look_up(c, 1)
                look_up(c, 2)
                look_up(c, 3)
                pairs(before, 0, first)
                look_up(c, 4)
                look_up(c, 5)
                pairs(before, 1, first)
                look_up(c, 6)
                layer1(before, 0, first)
                look_up(c, 7)
                transposes(c, 1, range(TR_BATCHES))
                layer1(before, 1, first)
                layer1(before, 2, first)
                layer1(before, 3, first)
                products(c, 0)
                layer2(before, 0, first)
                layer2(before, 1, first)
                products(c, 1)
                layer3(before, first)

            chunk(1, 0, True)
            with pe.Fori(2, CHUNKS) as c:
                chunk(c, c - 1, False)
            last = CHUNKS - 1
            for i in range(TILES):
                pairs(last, i, False)
            for n in range(N1):
                layer1(last, n, False)
            for n in range(N2):
                layer2(last, n, False)
            layer3(last, False)


def kernel(**inputs):
    import concourse.bacc as _bacc
    from concourse.bass_utils import run_bass_kernel_spmd as _run

    w1 = np.asarray(inputs["W_top1"])
    ids = np.asarray(inputs["ids"])
    arrays = {
        "dense": np.asarray(inputs["r_dense_features"]),
        "ids": ids,
        "ids_t": ids[:, HOT].T,
        "w1_dense": w1[:DIM],
        "w1_pairs": w1[DIM:DIM + PAIRS][pair_rows()],
        "w1_last": w1[DIM + PAIRS:],
        "b1": np.asarray(inputs["b_top1"]).reshape(N1, P).T,
        "w2": np.asarray(inputs["W_top2"]),
        "b2": np.asarray(inputs["b_top2"]).reshape(N2, P).T,
        "w3": np.asarray(inputs["W_top3"]).reshape(N2, P).T,
    }
    arrays |= {f"tbl_{t}": np.asarray(inputs[f"tbl_{t}"]) for t in range(TABLES)}
    arrays = {k: np.ascontiguousarray(a) for k, a in arrays.items()}

    nc = _bacc.Bacc("TRN2", target_bir_lowering=False, num_devices=1)
    ap = {k: nc.dram_tensor(f"in_{k}", a.shape, mybir.dt.from_np(a.dtype), kind="ExternalInput").ap()
          for k, a in arrays.items()}
    y = nc.dram_tensor("y", (1, BATCH), F32, kind="ExternalOutput").ap()
    build(nc, ap["dense"], ap["ids"], ap["ids_t"], [ap[f"tbl_{t}"] for t in range(TABLES)],
          ap["w1_dense"], ap["w1_pairs"], ap["w1_last"], ap["b1"], ap["w2"], ap["b2"], ap["w3"], y)
    r = _run(nc, [{f"in_{k}": a for k, a in arrays.items()}], core_ids=[0])
    return r.results[0]["y"].reshape(BATCH, 1)
```

```python
from contextlib import ExitStack

import concourse.bass as bass
from concourse import mybir
import numpy as np

F32 = mybir.dt.float32
F32R = mybir.dt.float32r
I32 = mybir.dt.int32
ALU = mybir.AluOpType
ACT = mybir.ActivationFunctionType

P = 128
BATCH = 2048
DIM = 128
ROWS = [12500, 12500, 1250, 1250, 1250, 12500, 1000, 12500, 1250, 1000, 1250, 1250, 12500, 125000,
        1000, 1000, 12500, 1000, 1000, 1000, 12500, 1000, 1250, 1000, 12500, 1250]
TABLES = len(ROWS)
VECS = TABLES + 1
UNIT = 2
KPARTS = 8
HOT_ROWS = 1000
HOT_P = HOT_ROWS // KPARTS
HOT = [t for t, r in enumerate(ROWS) if r == HOT_ROWS][1:]
GATHERED = [t for t in range(TABLES) if t not in HOT]
NG, NH = len(GATHERED), len(HOT)
NE = NG + 1
ORDER = [0] + [1 + t for t in GATHERED] + [1 + t for t in HOT]

TILES = 2
CHUNK = TILES * P
CHUNKS = BATCH // CHUNK
GROUP = 4
GROUPS = P // GROUP
OTHER = VECS - 1
GP, GN = GROUP * VECS, GROUP * OTHER
GROUPS_BANK = 4
BANKS = 4
GBATCHES = GROUPS // GROUPS_BANK
TR_BANK = 4
TR_BATCHES = -(-NE // TR_BANK)
HALF = GROUPS // 2
UNITS = NH * KPARTS // UNIT
RING = KPARTS // UNIT
STAGES = 3

WIN = OTHER // 2
ROW = VECS * OTHER
PAIRS = VECS * WIN
KT = 3
KP = PAIRS // KT
H1, H2 = 512, 256
N1 = H1 // P
ZROW = max(ROW, KT * H1 // TILES)
M_USES = TILES + N1 + TILES


def pair_rows():
    upper = {}
    for f in range(VECS):
        for g in range(f + 1, VECS):
            upper[f, g] = len(upper)
    rows = []
    for w in range(VECS):
        for j in range(WIN):
            at = (VECS * w + j) if w < VECS - 1 else WIN + j
            p, q = at // OTHER, at % OTHER + 1
            f, g = sorted((ORDER[p], ORDER[q]))
            rows.append(upper[f, g])
    assert sorted(rows) == list(range(len(upper)))
    return rows


def build(nc, dense, ids, ids_t, tables, w1_dense, w1_pairs, w1_last, b1, w2, b2, w3, y):
    ctx = ExitStack()
    with ctx:
        def sb(name, shape, dt=F32):
            return ctx.enter_context(nc.sbuf_tensor(name, shape, dt))

        def pb(name, shape):
            return ctx.enter_context(nc.psum_tensor(name, shape, F32))

        def sem(name):
            return ctx.enter_context(nc.semaphore(name))

        products_dram = nc.dram_tensor("products", (TILES, P, ROW), F32, kind="Internal").ap()

        tab_hi = sb("tab_hi", [P, NH, KPARTS, DIM], F32R)
        tab_lo = sb("tab_lo", [P, NH, KPARTS, DIM], F32R)
        row_of = sb("row_of", [P, KPARTS])
        row_of_i = sb("row_of_i", [P, KPARTS], I32)
        ident = sb("ident", [P, P])
        w1p = [sb(f"w1p_{x}", [P, KT, H1], F32R) for x in ("high", "low")]
        w1d = [sb(f"w1d_{x}", [P, H1], F32R) for x in ("high", "low")]
        w2s = [sb(f"w2_{x}", [P, N1, H2], F32R) for x in ("high", "low")]
        w3s = sb("w3s", [P, H2])
        b1s = sb("b1s", [P, N1])
        b2s = sb("b2s", [P, H2])
        idx = sb("idx", [P, TILES, TABLES], I32)
        emb = sb("emb", [P, TILES, NE, DIM])
        vec = sb("vec", [P, CHUNK, VECS])
        hot_ids = sb("hot_ids", [P, NH, CHUNK], I32)
        onehot = sb("onehot", [P, 2, KPARTS, CHUNK], F32R)
        prod = sb("prod", [P, GROUPS, GN])
        zrow = sb("zrow", [P, TILES, ZROW])
        zpair = sb("zpair", [P, TILES, PAIRS])
        z = [sb(f"z_{x}", [P, KT + 1, CHUNK], F32R) for x in ("high", "low")]
        h1 = sb("h1", [P, N1, CHUNK])
        h1s = [sb(f"h1_{x}", [P, N1, CHUNK], F32R) for x in ("high", "low")]
        h2 = sb("h2", [P, TILES, H2])
        ys = sb("ys", [P, TILES])
        w1p_in = zrow[0:KP, :, :].rearrange("p i r -> p (i r)")[:, 0:KT * H1].rearrange(
            "p (k n) -> p k n", n=H1)
        w1d_in = zpair[:, :, :].rearrange("p i r -> p (i r)")[:, 0:H1]
        w1e_in = h2[:, :, :].rearrange("p n b -> p (n b)")
        w2_in = h1[:, :, :]

        bank_ps = [pb(f"bank_ps{i}", [P, 512]) for i in range(BANKS)]
        hot_ps = [pb(f"hot_ps{i}", [P, 2, CHUNK]) for i in range(2)]
        mlp_ps = [pb(f"mlp_ps{i}", [P, 512]) for i in range(2)]

        idx_in = [sem(f"idx{i}_in") for i in range(TILES)]
        idx_known = sem("idx_known")
        zeroed = sem("zeroed")
        ident_set = sem("ident_set")
        numbered = sem("numbered")
        weights_in = sem("weights_in")
        tables_in = [sem(f"table{j}_in") for j in range(STAGES)]
        weights_added = sem("weights_added")
        weights_high = sem("weights_high")
        weights_low = sem("weights_low")
        row_of_set = sem("row_of_set")
        hi_set = sem("hi_set")
        lo_set = sem("lo_set")
        dense_in = [sem(f"dense{i}_in") for i in range(TILES)]
        emb_in = [sem(f"emb{i}_in") for i in range(TILES)]
        emb_free = sem("emb_free")
        tr_ready = sem("tr_ready")
        tr_copied = sem("tr_copied")
        hot_ids_free = sem("hot_ids_free")
        first_ids_in = sem("first_ids_in")
        hot_ids_in = sem("hot_ids_in")
        onehot_set = sem("onehot_set")
        looked_up = sem("looked_up")
        hot_copied = sem("hot_copied")
        prod_ready = sem("prod_ready")
        prod_copied = sem("prod_copied")
        prod_out = [sem(f"prod{h}_out") for h in range(2)]
        zrow_in = [sem(f"zrow{i}_in") for i in range(TILES)]
        dense_high = sem("dense_high")
        dense_low = sem("dense_low")
        z_high = sem("z_high")
        z_low = sem("z_low")
        h1_high = sem("h1_high")
        h1_low = sem("h1_low")
        pairs_packed = sem("pairs_packed")
        mlp_ready = sem("mlp_ready")
        h2_added = sem("h2_added")
        y_set = sem("y_set")
        y_out = sem("y_out")

        WEIGHT_LOADS = 7

        def prod_stage(j):
            return prod[0:HOT_P, :, :].rearrange("p g n -> p (g n)")[
                :, j % STAGES * KPARTS * DIM:(j % STAGES + 1) * KPARTS * DIM]

        block = ctx.enter_context(nc.Block())

        @block.sync
        def _(sp):
            def load_indices(c, i):
                sp.dma_start(idx[:, i, :], ids[bass.ds(c * CHUNK + i * P, P), :]
                             ).then_inc(idx_in[i], 16)

            def load_dense(c, i):
                sp.dma_start(emb[:, i, 0, :], dense[bass.ds(c * CHUNK + i * P, P), :]
                             ).then_inc(dense_in[i], 16)

            def load_hot_ids(at, j=0, end=NH):
                src = ids_t[j:end, bass.ds(at, CHUNK)]
                sp.dma_start(hot_ids[:, j:end, :], src.rearrange("(o f) b -> o f b", o=1)
                             .broadcast_to([P, end - j, CHUNK])
                             ).then_inc(hot_ids_in if end == NH else first_ids_in, 16)

            def load_table(j):
                src = tables[HOT[j]].rearrange("(p k) d -> p (k d)", k=KPARTS)
                for a, b in ((0, HOT_P // 16 * 16), (HOT_P // 16 * 16, HOT_P)):
                    sp.dma_start(prod_stage(j)[a:b, :], src[a:b, :]).then_inc(tables_in[j % STAGES], 16)

            load_indices(0, 0)
            load_hot_ids(0, 0, 2)
            load_table(0)
            load_hot_ids(0, 2, NH)
            load_indices(0, 1)
            load_table(1)
            load_table(2)
            load_dense(0, 0)
            load_dense(0, 1)
            for j in range(STAGES, NH):
                sp.wait_ge(lo_set, j - STAGES + 1)
                load_table(j)
            sp.dma_start(w1p_in, w1_pairs.rearrange("(k p) n -> p k n", k=KT)).then_inc(weights_in, 16)
            sp.dma_start(w1d_in, w1_dense).then_inc(weights_in, 16)
            sp.dma_start(w1e_in, w1_last).then_inc(weights_in, 16)
            sp.dma_start(w2_in, w2.rearrange("(k p) n -> p k n", k=N1)).then_inc(weights_in, 16)
            sp.dma_start(w3s[:, :], w3.broadcast_to([P, H2])).then_inc(weights_in, 16)
            sp.dma_start(b1s[:, :], b1).then_inc(weights_in, 16)
            sp.dma_start(b2s[:, :], b2.broadcast_to([P, H2])).then_inc(weights_in, 16)

            def store_products(c, i, h):
                sp.wait_ge(prod_copied, (c * TILES + i) * GBATCHES + (h + 1) * GBATCHES // 2)
                for s in range(GROUP):
                    dst = products_dram[i].rearrange("(t s) (v q) -> s v t q", s=GROUP, v=VECS)
                    sp.dma_start(dst[s, :, h * HALF:(h + 1) * HALF, :],
                                 prod[VECS * s:VECS * (s + 1), h * HALF:(h + 1) * HALF,
                                      s * OTHER:(s + 1) * OTHER]).then_inc(prod_out[h], 16)

            def load_rows(c, i, first=False):
                if first and i == 0:
                    sp.wait_ge(weights_low, 3)
                for h in range(2):
                    sp.wait_ge(prod_out[h], (c * TILES + i + 1) * GROUP * 16)
                sp.dma_start(zrow[:, i, 0:ROW], products_dram[i]).then_inc(zrow_in[i], 16)

            def store_result(c):
                for i in range(TILES):
                    sp.wait_ge(y_set, c * TILES + i + 1)
                    sp.dma_start(y[bass.ds(c * CHUNK + i * P, P), :], ys[:, i:i + 1]
                                 ).then_inc(y_out, 16)

            def chunk(c, first=False, to_load=2):
                if to_load:
                    sp.wait_ge(tr_ready, (c * TILES + 1) * TR_BATCHES)
                    load_dense(c + 1, 0)
                    sp.wait_ge(onehot_set, (c + 1) * UNITS)
                    sp.sem_inc(hot_ids_free, 1)
                    load_hot_ids((c + 1) * CHUNK)
                store_products(c, 0, 0)
                store_products(c, 0, 1)
                if to_load:
                    sp.wait_ge(emb_in[1], (c + 1) * NG * 16)
                    load_indices(c + 1, 1)
                load_rows(c, 0, first)
                if to_load:
                    sp.wait_ge(tr_ready, (c * TILES + 2) * TR_BATCHES)
                    load_dense(c + 1, 1)
                store_products(c, 1, 0)
                store_products(c, 1, 1)
                load_rows(c, 1)
                if to_load > 1:
                    sp.wait_ge(emb_in[0], (c + 2) * NG * 16)
                    load_indices(c + 2, 0)
                if not first:
                    store_result(c - 1)

            sp.wait_ge(emb_in[0], NG * 16)
            load_indices(1, 0)
            chunk(0, first=True)
            with sp.Fori(1, CHUNKS - 2) as c:
                chunk(c)
            chunk(CHUNKS - 2, to_load=1)
            chunk(CHUNKS - 1, to_load=0)
            store_result(CHUNKS - 1)
            sp.wait_ge(y_out, CHUNKS * TILES * 16)

        @block.gpsimd
        def _(pool):
            pool.iota(row_of_i[:, :], pattern=[[1, KPARTS]], base=0,
                      channel_multiplier=KPARTS).then_inc(numbered, 1)

            def gathers(c, first):
                for i in range(TILES):
                    if not first:
                        pool.wait_ge(tr_ready, ((c - 1) * TILES + i + 1) * TR_BATCHES)
                        pool.sem_inc(emb_free, 1)
                    pool.wait_ge(idx_in[i], (c + 1) * 16)
                    pool.sem_inc(idx_known, 1)
                    for n, t in enumerate(GATHERED):
                        nc.gpsimd.indirect_dma_start(
                            emb[:, i, 1 + n, :], None, tables[t],
                            bass.IndirectOffsetOnAxis(idx[:, i, t:t + 1], 0)).then_inc(emb_in[i], 16)

            def make_ident():
                nc.gpsimd.memset(ident[:, :], 0.0).then_inc(zeroed, 1)
                pool.wait_ge(zeroed, 1)
                nc.gpsimd.affine_select(out=ident[:, :], in_=ident[:, :], compare_op=ALU.not_equal,
                                        fill=1.0, base=0, pattern=[[-1, P]], channel_multiplier=1
                                        ).then_inc(ident_set, 1)

            make_ident()
            gathers(0, True)
            with pool.Fori(1, CHUNKS) as c:
                gathers(c, False)

        @block.vector
        def _(dve):
            dve.wait_ge(numbered, 1)
            nc.vector.tensor_copy(row_of[:, :], row_of_i[:, :]).then_inc(row_of_set, 1)
            dve.wait_ge(row_of_set, 1)

            def low_table(j):
                dve.wait_ge(hi_set, j + 1)
                nc.vector.tensor_tensor(
                    tab_lo[0:HOT_P, j, :, :].rearrange("p k d -> p (k d)"), prod_stage(j),
                    tab_hi[0:HOT_P, j, :, :].rearrange("p k d -> p (k d)"), ALU.subtract
                ).then_inc(lo_set, 1)

            def low_weights():
                dve.wait_ge(weights_high, 3)
                nc.vector.tensor_tensor(w1p[1][0:KP, :, :], w1p_in, w1p[0][0:KP, :, :], ALU.subtract
                                        ).then_inc(weights_low, 1)
                nc.vector.tensor_tensor(w1d[1][:, :], w1d_in, w1d[0][:, :], ALU.subtract
                                        ).then_inc(weights_low, 1)
                nc.vector.tensor_tensor(w2s[1][:, :, :], w2_in, w2s[0][:, :, :], ALU.subtract
                                        ).then_inc(weights_low, 1)

            def one_hots(c, j, first=False):
                for u in range(RING):
                    if not (first and j < 2):
                        dve.wait_ge(looked_up, c * UNITS + (j - 2) * RING + u + 1)
                    for k in range(u * UNIT, (u + 1) * UNIT):
                        last = nc.vector.tensor_scalar(
                            onehot[0:HOT_P, j % 2, k, :], hot_ids[0:HOT_P, j, :],
                            row_of[0:HOT_P, k:k + 1], None, ALU.is_equal)
                    last.then_inc(onehot_set, 1)

            def pack_pairs(c, i):
                dve.wait_ge(zrow_in[i], (c + 1) * 16)
                nc.vector.tensor_copy(
                    zpair[:, i, 0:ROW // 2].rearrange("b (w j) -> b w j", j=WIN)[:, 0:OTHER],
                    zrow[:, i, 0:ROW].rearrange("b (w v) -> b w v", v=VECS)[:, :, 0:WIN])
                nc.vector.tensor_copy(zpair[:, i, OTHER * WIN:PAIRS], zrow[:, i, WIN:2 * WIN]
                                      ).then_inc(pairs_packed, 1)

            def low_pairs(c, i):
                dve.wait_ge(z_high, c * TILES + i + 1)
                at = slice(i * P, (i + 1) * P)
                nc.vector.tensor_tensor(
                    z[1][0:KP, 0:KT, at], mlp_ps[i % 2][0:KP, 0:KT * P].rearrange("p (k b) -> p k b", b=P),
                    z[0][0:KP, 0:KT, at], ALU.subtract).then_inc(z_low, 1)

            def low_dense(c):
                dve.wait_ge(dense_high, c + 1)
                nc.vector.tensor_tensor(z[1][:, KT, :], vec[:, :, 0], z[0][:, KT, :], ALU.subtract
                                        ).then_inc(dense_low, 1)

            def low_h1(c, n):
                dve.wait_ge(h1_high, c * N1 + n + 1)
                nc.vector.tensor_tensor(h1s[1][:, n, :], h1[:, n, :], h1s[0][:, n, :], ALU.subtract
                                        ).then_inc(h1_low, 1)

            dve.wait_ge(first_ids_in, 16)
            def result(c, i, first=False):
                dve.wait_ge(mlp_ready, c * M_USES + TILES + N1 + i + 1)
                nc.vector.tensor_tensor(h2[:, i, :], mlp_ps[i][:, 0:H2], b2s[:, :], ALU.add
                                        ).then_inc(h2_added, 1)
                dve.wait_ge(h2_added, c * TILES + i + 1)
                if i == 0 and not first:
                    dve.wait_ge(y_out, c * TILES * 16)
                nc.vector.scalar_tensor_tensor(h2[:, i, :], h2[:, i, :], 0.0, w3s[:, :], ALU.max,
                                               ALU.mult, accum_out=ys[:, i:i + 1]).then_inc(y_set, 1)

            for j in range(NH):
                if j == 2:
                    dve.wait_ge(hot_ids_in, 16)
                one_hots(0, j, True)
                low_table(j)
            dve.wait_ge(weights_in, WEIGHT_LOADS * 16)
            nc.vector.tensor_tensor(w1d_in, w1d_in, w1e_in, ALU.add).then_inc(weights_added, 1)

            def chunk(c, first=False):
                before = c - 1
                dve.wait_ge(hot_ids_in, (c + 1) * 16)
                for j in range(2):
                    one_hots(c, j)
                low_dense(before)
                if first:
                    low_weights()
                for j in range(2, 4):
                    one_hots(c, j)
                pack_pairs(before, 0)
                one_hots(c, 4)
                pack_pairs(before, 1)
                one_hots(c, 5)
                low_pairs(before, 0)
                one_hots(c, 6)
                low_pairs(before, 1)
                one_hots(c, 7)
                for n in range(N1):
                    low_h1(before, n)
                for i in range(TILES):
                    result(before, i, first)

            chunk(1, True)
            with dve.Fori(2, CHUNKS) as c:
                chunk(c)
            last = CHUNKS - 1
            low_dense(last)
            for i in range(TILES):
                pack_pairs(last, i)
                low_pairs(last, i)
            for n in range(N1):
                low_h1(last, n)
            for i in range(TILES):
                result(last, i)

        @block.scalar
        def _(act):
            def high_table(j):
                act.wait_ge(tables_in[j % STAGES], (j // STAGES + 1) * 2 * 16)
                nc.scalar.activation(tab_hi[0:HOT_P, j, :, :].rearrange("p k d -> p (k d)"),
                                     prod_stage(j), ACT.Copy).then_inc(hi_set, 1)

            def copy_vectors(c, i, first=False):
                if i == 0 and not first:
                    act.wait_ge(dense_low, c)
                for k in range(TR_BATCHES):
                    n = min(TR_BANK, NE - k * TR_BANK)
                    act.wait_ge(tr_ready, (c * TILES + i) * TR_BATCHES + k + 1)
                    nc.scalar.activation(
                        vec[:, i * P:(i + 1) * P, k * TR_BANK:k * TR_BANK + n].rearrange("d b v -> d v b"),
                        bank_ps[k % BANKS][:, 0:n * P].rearrange("d (v b) -> d v b", b=P), ACT.Copy
                    ).then_inc(tr_copied, 1)

            def copy_looked_up(c, q):
                act.wait_ge(looked_up, c * UNITS + 2 * (q + 1) * RING)
                nc.scalar.activation(vec[:, :, NE + 2 * q:NE + 2 * q + 2].rearrange("d b v -> d v b"),
                                     hot_ps[q % 2][:, :, :], ACT.Copy).then_inc(hot_copied, 1)

            def high_weights():
                act.wait_ge(weights_in, WEIGHT_LOADS * 16)
                nc.scalar.activation(w1p[0][0:KP, :, :], w1p_in, ACT.Copy).then_inc(weights_high, 1)
                nc.scalar.activation(w2s[0][:, :, :], w2_in, ACT.Copy).then_inc(weights_high, 1)
                act.wait_ge(weights_added, 1)
                nc.scalar.activation(w1d[0][:, :], w1d_in, ACT.Copy).then_inc(weights_high, 1)

            def copy_products(c, i, first=False):
                for k in range(GBATCHES):
                    if k % (GBATCHES // 2) == 0 and not (first and i == 0):
                        act.wait_ge(prod_out[k // (GBATCHES // 2)], (c * TILES + i) * GROUP * 16)
                    act.wait_ge(prod_ready, (c * TILES + i) * GBATCHES + k + 1)
                    nc.scalar.activation(
                        prod[0:GP, k * GROUPS_BANK:(k + 1) * GROUPS_BANK, :],
                        bank_ps[k % BANKS][0:GP, 0:GROUPS_BANK * GN].rearrange(
                            "p (g n) -> p g n", n=GN),
                        ACT.Copy).then_inc(prod_copied, 1)

            def mlp_use(c, u):
                act.wait_ge(mlp_ready, c * M_USES + u + 1)
                return mlp_ps[u % 2]

            def high_pairs(c, i):
                ps = mlp_use(c, i)
                nc.scalar.activation(z[0][0:KP, 0:KT, i * P:(i + 1) * P],
                                     ps[0:KP, 0:KT * P].rearrange("p (k b) -> p k b", b=P), ACT.Copy
                                     ).then_inc(z_high, 1)

            def high_dense(c):
                act.wait_ge(tr_copied, (c + 1) * TILES * TR_BATCHES)
                nc.scalar.activation(z[0][:, KT, :], vec[:, :, 0], ACT.Copy).then_inc(dense_high, 1)

            def layer1(c, n):
                ps = mlp_use(c, TILES + n)
                nc.scalar.activation(h1[:, n, :], ps[:, 0:CHUNK], ACT.Relu, bias=b1s[:, n:n + 1])
                nc.scalar.activation(h1s[0][:, n, :], ps[:, 0:CHUNK], ACT.Relu, bias=b1s[:, n:n + 1]
                                     ).then_inc(h1_high, 1)

            for j in range(2):
                high_table(j)
            for q in range(NH // 2):
                for j in range(2 * q + 2, min(2 * q + 4, NH)):
                    high_table(j)
                if q == NH // 2 - 1:
                    copy_vectors(0, 0, first=True)
                copy_looked_up(0, q)
            act.wait_ge(lo_set, NH)
            copy_products(0, 0, True)
            high_weights()
            copy_vectors(0, 1)
            high_dense(0)
            copy_products(0, 1, True)
            act.wait_ge(weights_low, 3)

            def chunk(c, before, last=False):
                copy_looked_up(c, 0)
                copy_looked_up(c, 1)
                high_pairs(before, 0)
                copy_vectors(c, 0)
                copy_looked_up(c, 2)
                high_pairs(before, 1)
                if not last:
                    layer1(before, 0)
                copy_looked_up(c, 3)
                if not last:
                    for n in range(1, N1):
                        layer1(before, n)
                copy_products(c, 0)
                copy_vectors(c, 1)
                if last:
                    layer1(before, 0)
                else:
                    high_dense(c)
                copy_products(c, 1)
                if last:
                    for n in range(1, N1):
                        layer1(before, n)
                    high_dense(c)

            chunk(1, 0)
            with act.Fori(2, CHUNKS - 1) as c:
                chunk(c, c - 1)
            last = CHUNKS - 1
            chunk(last, last - 1, last=True)
            for i in range(TILES):
                high_pairs(last, i)
            for n in range(N1):
                layer1(last, n)

        @block.tensor
        def _(pe):
            def transposes(c, i, first=False):
                pe.wait_ge(dense_in[i], (c + 1) * 16)
                pe.wait_ge(emb_in[i], (c + 1) * NG * 16)
                for k in range(TR_BATCHES):
                    if k >= BANKS:
                        pe.wait_ge(tr_copied, (c * TILES + i) * TR_BATCHES + k - BANKS + 1)
                    elif not first:
                        pe.wait_ge(prod_copied, (c * TILES + i) * GBATCHES - BANKS + k + 1)
                    for n in range(k * TR_BANK, min((k + 1) * TR_BANK, NE)):
                        at = n % TR_BANK * P
                        last = nc.tensor.transpose(bank_ps[k % BANKS][:, at:at + P], emb[:, i, n, :],
                                                   ident[:, :])
                    last.then_inc(tr_ready, 1)

            def look_up(c, j, first=False):
                if first:
                    pe.wait_ge(lo_set, j + 1)
                if j % 2 == 0 and not (first and j < 4):
                    pe.wait_ge(hot_copied, c * (NH // 2) + j // 2 - 1)
                out = hot_ps[j // 2 % 2][:, j % 2, :]
                for k in range(KPARTS):
                    if k % UNIT == 0:
                        pe.wait_ge(onehot_set, c * UNITS + j * RING + k // UNIT + 1)
                    for part, tab in enumerate((tab_hi, tab_lo)):
                        last = nc.tensor.matmul(out, tab[0:HOT_P, j, k, :], onehot[0:HOT_P, j % 2, k, :],
                                                start=(k == 0 and part == 0),
                                                stop=(k == KPARTS - 1 and part == 1))
                    if k % UNIT == UNIT - 1:
                        last.then_inc(looked_up, 1)

            def products(c, i):
                if i == 0:
                    pe.wait_ge(hot_copied, (c + 1) * (NH // 2))
                pe.wait_ge(tr_copied, (c * TILES + i + 1) * TR_BATCHES)
                for k in range(GBATCHES):
                    if k >= BANKS:
                        pe.wait_ge(prod_copied, (c * TILES + i) * GBATCHES + k - BANKS + 1)
                    for g in range(GROUPS_BANK):
                        b = i * P + (k * GROUPS_BANK + g) * GROUP
                        last = nc.tensor.matmul(
                            bank_ps[k % BANKS][0:GP, g * GN:(g + 1) * GN],
                            vec[:, b:b + GROUP, :].rearrange("d b v -> d (b v)"),
                            vec[:, b:b + GROUP, 1:VECS], start=True, stop=True)
                    last.then_inc(prod_ready, 1)

            def mlp_bank(c, u, first):
                if u < TILES:
                    if not first:
                        pe.wait_ge(h2_added, c * TILES)
                elif u < 2 * TILES:
                    pe.wait_ge(z_low, c * TILES + u - TILES + 1)
                else:
                    pe.wait_ge(h1_high, c * N1 + u - TILES - 1)
                return mlp_ps[u % 2]

            def pairs(c, i, first=False):
                pe.wait_ge(pairs_packed, c * TILES + i + 1)
                ps = mlp_bank(c, i, first)
                for k in range(KT):
                    last = nc.tensor.transpose(ps[0:KP, k * P:(k + 1) * P],
                                               zpair[:, i, k * KP:(k + 1) * KP], ident[:, :])
                last.then_inc(mlp_ready, 1)

            WITH_HIGH, WITH_LOW = ((0, 0), (1, 0)), ((0, 1),)

            def layer1(c, n, first=False):
                if first and n == 0:
                    pe.wait_ge(weights_low, 3)
                if n == 0:
                    pe.wait_ge(dense_low, c + 1)
                ps = mlp_bank(c, TILES + n, first)
                steps = ([(KT, t) for t in WITH_HIGH + WITH_LOW]
                         + [(k, t) for k in range(KT) for t in WITH_HIGH]
                         + [(k, t) for k in range(KT) for t in WITH_LOW])
                for m, (k, (a, b)) in enumerate(steps):
                    if n == 0 and m == 3:
                        pe.wait_ge(z_high, (c + 1) * TILES)
                    if n == 0 and m == 3 + 2 * KT:
                        pe.wait_ge(z_low, (c + 1) * TILES)
                    rows = KP if k < KT else P
                    w = (w1p[a][0:KP, k, n * P:(n + 1) * P] if k < KT else
                         w1d[a][:, n * P:(n + 1) * P])
                    last = nc.tensor.matmul(ps[:, 0:CHUNK], w, z[b][0:rows, k, :], start=(m == 0),
                                            stop=(m == len(steps) - 1))
                last.then_inc(mlp_ready, 1)

            def layer2(c, i, first=False):
                ps = mlp_bank(c, TILES + N1 + i, first)
                steps = ([(k, t) for k in range(N1) for t in WITH_HIGH]
                         + [(k, t) for k in range(N1) for t in WITH_LOW])
                for m, (k, (a, b)) in enumerate(steps):
                    if i == 0 and m == 2 * (N1 - 1):
                        pe.wait_ge(h1_high, (c + 1) * N1)
                    if i == 0 and m >= 2 * N1:
                        pe.wait_ge(h1_low, c * N1 + k + 1)
                    last = nc.tensor.matmul(ps[:, 0:H2], h1s[b][:, k, i * P:(i + 1) * P],
                                            w2s[a][:, k, :], start=(m == 0),
                                            stop=(m == len(steps) - 1))
                last.then_inc(mlp_ready, 1)

            for j in range(NH):
                if j == NH - 2:
                    pe.wait_ge(ident_set, 1)
                    transposes(0, 0, True)
                look_up(0, j, True)
            products(0, 0)
            look_up(1, 0)
            transposes(0, 1)
            look_up(1, 1)
            products(0, 1)

            def chunk(c, before, first=False, last=False):
                for j in range(2 if first else 0, 4):
                    look_up(c, j)
                if first:
                    look_up(c, 4)
                    pairs(before, 0, first)
                    transposes(c, 0)
                else:
                    pairs(before, 0, first)
                    transposes(c, 0)
                    look_up(c, 4)
                look_up(c, 5)
                pairs(before, 1, first)
                look_up(c, 6)
                if not last:
                    layer1(before, 0, first)
                look_up(c, 7)
                if not last:
                    for n in range(1, N1):
                        layer1(before, n, first)
                products(c, 0)
                transposes(c, 1)
                if last:
                    layer1(before, 0)
                    products(c, 1)
                    for n in range(1, N1):
                        layer1(before, n)
                for i in range(TILES):
                    layer2(before, i, first)
                if not last:
                    products(c, 1)

            chunk(1, 0, first=True)
            with pe.Fori(2, CHUNKS - 1) as c:
                chunk(c, c - 1)
            last = CHUNKS - 1
            chunk(last, last - 1, last=True)
            for i in range(TILES):
                pairs(last, i)
            for n in range(N1):
                layer1(last, n)
            for i in range(TILES):
                layer2(last, i)


def kernel(**inputs):
    import concourse.bacc as _bacc
    from concourse.bass_utils import run_bass_kernel_spmd as _run

    w1 = np.asarray(inputs["W_top1"])
    ids = np.asarray(inputs["ids"])
    arrays = {
        "dense": np.asarray(inputs["r_dense_features"]),
        "ids": ids,
        "ids_t": ids[:, HOT].T,
        "w1_dense": w1[:DIM],
        "w1_pairs": w1[DIM:DIM + PAIRS][pair_rows()],
        "w1_last": w1[DIM + PAIRS:],
        "b1": np.asarray(inputs["b_top1"]).reshape(N1, P).T,
        "w2": np.asarray(inputs["W_top2"]),
        "b2": np.asarray(inputs["b_top2"]).reshape(1, H2),
        "w3": np.asarray(inputs["W_top3"]).reshape(1, H2),
    }
    arrays |= {f"tbl_{t}": np.asarray(inputs[f"tbl_{t}"]) for t in range(TABLES)}
    arrays = {k: np.ascontiguousarray(a) for k, a in arrays.items()}

    nc = _bacc.Bacc("TRN2", target_bir_lowering=False, num_devices=1)
    ap = {k: nc.dram_tensor(f"in_{k}", a.shape, mybir.dt.from_np(a.dtype), kind="ExternalInput").ap()
          for k, a in arrays.items()}
    y = nc.dram_tensor("y", (BATCH, 1), F32, kind="ExternalOutput").ap()
    build(nc, ap["dense"], ap["ids"], ap["ids_t"], [ap[f"tbl_{t}"] for t in range(TABLES)],
          ap["w1_dense"], ap["w1_pairs"], ap["w1_last"], ap["b1"], ap["w2"], ap["b2"], ap["w3"], y)
    r = _run(nc, [{f"in_{k}": a for k, a in arrays.items()}], core_ids=[0])
    return r.results[0]["y"]
```
